# Optimizing a Trainium2 kernel written in Bass

```python
import numpy as np
import jax
import jax.numpy as jnp

def _softmax(x, axis=-1):
    return jax.nn.softmax(x, axis=axis)

def _gelu(x):
    return jax.nn.gelu(x, approximate=True)

def _silu(x):
    return jax.nn.silu(x)

def _sigmoid(x):
    return jax.nn.sigmoid(x)

def _layernorm(x, axis=-1, eps=1e-05):
    m = jnp.mean(x, axis=axis, keepdims=True)
    v = jnp.var(x, axis=axis, keepdims=True)
    return (x - m) / jnp.sqrt(v + eps)

def _scatter_add(tgt, idx, src, axis=0):
    return tgt.at[idx].add(src)

def _segment_sum(src, seg, n):
    return jax.ops.segment_sum(src, seg, n)
kernel_name = 'mk_cond_resid_d2_seqx_r2_b08f0a'

def setup_inputs(seed: int=0):
    np.random.seed(seed)
    _w = jnp.asarray

    def _rec_inputs():
        import jax
        import jax.numpy as jnp
        _rk = jax.random.key(seed)
        x = -0.0003929 + 0.9999 * jax.random.normal(jax.random.fold_in(_rk, 1), (128, 128, 512), jnp.float32)
        _lenS = 128 - jax.random.randint(jax.random.fold_in(_rk, 7), (128,), 0, max(1, 128 // 4) + 1, jnp.int32)
        _lenS2 = 128 - jax.random.randint(jax.random.fold_in(_rk, 8), (128,), 0, max(1, 128 // 4) + 1, jnp.int32)
        cond_1024 = 0.00061147 + 0.102565 * jax.random.normal(jax.random.fold_in(_rk, 11), (128, 512), jnp.float32)
        return (x, cond_1024)
    x, cond_1024 = _rec_inputs()

    def _L0_cond_setup():
        import jax, jax.numpy as jnp
        import numpy as np
        key = jax.random.key(seed)
        ks = jax.random.split(key, 8)
        B, L, D, N, K = (4, 2048, 512, 64, 4)
        return {'x': jax.random.normal(ks[0], (B, L, D), dtype=jnp.float32), 'conv_w': jax.random.normal(ks[1], (K, 1, D), dtype=jnp.float32) * 0.1, 'conv_b': jnp.zeros((D,), dtype=jnp.float32), 'Wp': jax.random.normal(ks[2], (D, 2 * N), dtype=jnp.float32) * (1.0 / np.sqrt(D)), 'bp': jnp.zeros((2 * N,), dtype=jnp.float32), 'Ws': jax.random.normal(ks[3], (D, N), dtype=jnp.float32) * (1.0 / np.sqrt(D)), 'bs': jnp.zeros((N,), dtype=jnp.float32), 'A_log': jax.random.normal(ks[4], (N,), dtype=jnp.float32) * 0.02, 'dt_log': jax.random.normal(ks[5], (N,), dtype=jnp.float32) * 0.02, 'Wo': jax.random.normal(ks[6], (N, D), dtype=jnp.float32) * (1.0 / np.sqrt(N)), 'bo': jnp.zeros((D,), dtype=jnp.float32)}
    _L0_cond_all = _L0_cond_setup()
    _L0_cond_in = {k: v for k, v in _L0_cond_all.items() if k in ('conv_b', 'Wp', 'bp', 'Ws', 'bs', 'A_log', 'dt_log', 'Wo', 'bo')}
    del _L0_cond_all

    def _L1_cond_setup():
        import jax, jax.numpy as jnp
        import numpy as np
        N, T, D, H = (128, 256, 512, 512)
        key = jax.random.key(seed)
        k1, k2, k3, k4 = jax.random.split(key, 4)
        x = jax.random.normal(k1, (N, T, D), dtype=jnp.float32)
        h0 = jax.random.normal(k2, (N, H), dtype=jnp.float32)
        Wx = jax.random.normal(k3, (D, H), dtype=jnp.float32) / np.sqrt(D)
        Wh = jax.random.normal(k4, (H, H), dtype=jnp.float32) / np.sqrt(H)
        b = jnp.zeros((H,), dtype=jnp.float32)
        return {'x': x, 'h0': h0, 'Wx': Wx, 'Wh': Wh, 'b': b}
    _L1_cond_all = _L1_cond_setup()
    _L1_cond_in = {k: v for k, v in _L1_cond_all.items() if k in ('Wx', 'Wh', 'b')}
    del _L1_cond_all
    return {'x': x, 'cond_1024': cond_1024, 'L0_cond_conv_b': _L0_cond_in['conv_b'], 'L0_cond_Wp': _L0_cond_in['Wp'], 'L0_cond_bp': _L0_cond_in['bp'], 'L0_cond_Ws': _L0_cond_in['Ws'], 'L0_cond_bs': _L0_cond_in['bs'], 'L0_cond_A_log': _L0_cond_in['A_log'], 'L0_cond_dt_log': _L0_cond_in['dt_log'], 'L0_cond_Wo': _L0_cond_in['Wo'], 'L0_cond_bo': _L0_cond_in['bo'], 'L1_cond_Wx': _L1_cond_in['Wx'], 'L1_cond_Wh': _L1_cond_in['Wh'], 'L1_cond_b': _L1_cond_in['b']}

def reference(x, cond_1024, L0_cond_conv_b, L0_cond_Wp, L0_cond_bp, L0_cond_Ws, L0_cond_bs, L0_cond_A_log, L0_cond_dt_log, L0_cond_Wo, L0_cond_bo, L1_cond_Wx, L1_cond_Wh, L1_cond_b):
    import jax
    import jax.numpy as jnp

    def _L0_cond_ref(x, conv_w, conv_b, Wp, bp, Ws, bs, A_log, dt_log, Wo, bo):
        import jax, jax.numpy as jnp
        import numpy as np
        B, L, D = x.shape
        K = conv_w.shape[0]
        N = Ws.shape[1]
        x_pad = jnp.pad(x, ((0, 0), (K - 1, 0), (0, 0)))
        conv = conv_b + sum((x_pad[:, k:k + L, :] * conv_w[k, 0] for k in range(K)))
        proj = conv @ Wp + bp
        B_t = jax.nn.softplus(proj[..., :N])
        C_t = jnp.tanh(proj[..., N:])
        u = x @ Ws + bs
        A = -jax.nn.softplus(A_log)
        dt = jax.nn.softplus(dt_log)
        decay = 1.0 + dt * A

        def step(state, inputs):
            u_t, b_t, c_t = inputs
            state = decay * state + dt * b_t * u_t
            return (state, c_t * state)
        init = jnp.zeros((B, N), dtype=x.dtype)
        xs = tuple((jnp.swapaxes(a, 0, 1) for a in (u, B_t, C_t)))
        _, ys = jax.lax.scan(step, init, xs, unroll=4)
        y = jnp.swapaxes(ys, 0, 1)
        return y @ Wo + bo

    def _L1_cond_ref(x, h0, Wx, Wh, b):
        import jax, jax.numpy as jnp
        import numpy as np
        N, T, D, H = (128, 256, 512, 512)
        xW = jnp.einsum('ntd,dh->tnh', x, Wx) + b

        def step(h, xw_t):
            h_next = jnp.tanh(h @ Wh + xw_t)
            return (h_next, h_next)
        _, hs = jax.lax.scan(step, h0, xW)
        return jnp.swapaxes(hs, 0, 1)
    x = x + _L0_cond_ref(x, cond_1024[:, None, :], L0_cond_conv_b, L0_cond_Wp, L0_cond_bp, L0_cond_Ws, L0_cond_bs, L0_cond_A_log, L0_cond_dt_log, L0_cond_Wo, L0_cond_bo)
    x = x + _L1_cond_ref(x, cond_1024, L1_cond_Wx, L1_cond_Wh, L1_cond_b)
    return x

_drawn_inputs = setup_inputs


def setup_inputs(seed=0):
    import zlib

    import numpy as np

    out = dict(_drawn_inputs(seed))
    spreads = {'L0_cond_conv_b': (0.0, 0.1),
     'L0_cond_bp': (0.0, 0.1),
     'L0_cond_bs': (0.0, 0.1),
     'L0_cond_bo': (0.0, 0.1),
     'L1_cond_b': (0.0, 0.1)}
    factors = {'L0_cond_A_log': 8.0, 'L0_cond_dt_log': 8.0}
    for name, (base, spread) in spreads.items():
        noise = np.random.default_rng([zlib.crc32(name.encode()), seed]).standard_normal(out[name].shape)
        drawn = base * np.exp(spread * noise) if base else spread * noise
        out[name] = jnp.asarray(drawn.astype(out[name].dtype))
    for name, factor in factors.items():
        out[name] = (out[name] * factor).astype(out[name].dtype)
    return out
```

```python
from contextlib import ExitStack

import concourse.bass as bass
from concourse import mybir

F32 = mybir.dt.float32
F32R = mybir.dt.float32r
ALU = mybir.AluOpType
ACT = mybir.ActivationFunctionType

BATCH = 128
TIME = 128
D = 512
N = 64
P = 128
KC = D // P
RING = 8
CH = 8
PER_BANK = 4
LOADS = D // CH
BANKS = P // PER_BANK
G = 4
GROUPS = TIME // G
SOFT = 8
DMA = 16


def wait(engine, sem, value):
    if not isinstance(value, int) or value > 0:
        engine.wait_ge(sem, value)


def build(nc, x_rev, x_dtb, hankel, h0_t, conv_b, Wp, bp, Ws, bs, A_log, dt_log, Wo, bo, Wx, Wh, b, out):
    ctx = ExitStack()
    with ctx:
        def sb(stack, name, shape, dt=F32):
            return stack.enter_context(nc.sbuf_tensor(name, shape, dt))

        def sem(name):
            return ctx.enter_context(nc.semaphore(name))

        bank = [ctx.enter_context(nc.psum_tensor(f"bank{i}", [P, 512], F32)) for i in range(8)]
        CONV, TURN, PROJ = bank[0:4], bank[4:6], bank[6:8]
        ZB, HB, XB, UB = bank[0:2], bank[2:4], bank[4:6], bank[6]

        bc = sb(ctx, "bc", [P, TIME * BATCH])
        ident = sb(ctx, "ident", [P, P])
        wp_now = sb(ctx, "wp_now", [P, P + 1])
        turned = sb(ctx, "turned", [P, 2, 512])
        bp_c = sb(ctx, "bp_c", [P, 1])
        bo_c = sb(ctx, "bo_c", [P, KC])
        bs_c = sb(ctx, "bs_c", [N, 1])
        rates = sb(ctx, "rates", [P, 6])
        rates_e = sb(ctx, "rates_e", [P, 2])
        ws_f = sb(ctx, "ws_f", [P, KC, N])
        ws_hl = sb(ctx, "ws_hl", [P, KC, 2 * N], F32R)
        wo_f = sb(ctx, "wo_f", [P, D])
        wo_hi = sb(ctx, "wo_hi", [P, D], F32R)
        wo_lo = sb(ctx, "wo_lo", [P, D], F32R)

        with ExitStack() as first:
            t_ring = sb(first, "t_ring", [P, RING, CH, TIME])
            x_ring = sb(first, "x_ring", [P, RING, CH, BATCH])
            conv = sb(first, "conv", [P, TIME, P])
        wx_hi = sb(ctx, "wx_hi", [P, KC, D], F32R)
        wx_lo = sb(ctx, "wx_lo", [P, KC, D], F32R)
        wh_hi = sb(ctx, "wh_hi", [P, KC, D], F32R)
        wh_lo = sb(ctx, "wh_lo", [P, KC, D], F32R)
        w_f = sb(ctx, "w_f", [P, KC, D])
        bias_f = sb(ctx, "bias_f", [P, D])
        bias_hl = sb(ctx, "bias_hl", [P, D], F32R)
        h0_f = sb(ctx, "h0_f", [P, KC, BATCH])
        ones = sb(ctx, "ones", [P, P], F32R)
        x_f = sb(ctx, "x_f", [P, 2, KC, G, BATCH])
        x_hi = sb(ctx, "x_hi", [P, KC, G, BATCH], F32R)
        x_lo = sb(ctx, "x_lo", [P, KC, G, BATCH], F32R)
        x1_f = sb(ctx, "x1_f", [P, 2, KC, G, BATCH])
        x1_hi = sb(ctx, "x1_hi", [P, KC, G, BATCH], F32R)
        x1_lo = sb(ctx, "x1_lo", [P, KC, G, BATCH], F32R)
        hT_hi = sb(ctx, "hT_hi", [P, KC, BATCH], F32R)
        hT_lo = sb(ctx, "hT_lo", [P, KC, BATCH], F32R)
        h_f = sb(ctx, "h_f", [P, D])
        u_lo = sb(ctx, "u_lo", [N, G * BATCH])
        u_sum = sb(ctx, "u_sum", [N, G * BATCH])
        v_f = sb(ctx, "v_f", [P, G, BATCH])
        s_f = sb(ctx, "s_f", [P, G, BATCH])
        y_f = sb(ctx, "y_f", [P, G * BATCH])
        y_hl = sb(ctx, "y_hl", [P, G * BATCH], F32R)

        soft = [x1_f[0:N, i, :, :, :].rearrange("p c t b -> p (c t b)") for i in range(2)]
        PIECE = TIME * BATCH // SOFT

        def f(ap):
            return ap.bitcast(F32)

        ring_loaded = [sem(f"ring_loaded{i}") for i in range(RING)]
        conv_done = sem("conv_done")
        conv_copied_act = sem("conv_copied_act")
        conv_copied_dve = sem("conv_copied_dve")
        turn_done = sem("turn_done")
        turn_copied = sem("turn_copied")
        wp_loaded = sem("wp_loaded")
        proj_done = sem("proj_done")
        proj_added = sem("proj_added")
        ident_zero = sem("ident_zero")
        ident_ready = sem("ident_ready")
        bp_loaded = sem("bp_loaded")
        small_loaded = sem("small_loaded")
        rate_step = sem("rate_step")
        rate_act = sem("rate_act")
        wo_scaled = sem("wo_scaled")
        wx_loaded = sem("wx_loaded")
        wh_loaded = sem("wh_loaded")
        late_loaded = sem("late_loaded")
        pool_step = sem("pool_step")
        weights_ready = sem("weights_ready")
        abs_ready = sem("abs_ready")
        exp_ready = sem("exp_ready")
        ln_ready = sem("ln_ready")
        b_ready = sem("b_ready")
        x_loaded = [sem(f"x_loaded{i}") for i in range(2)]
        xhi_ready = sem("xhi_ready")
        xlo_ready = sem("xlo_ready")
        u_done = sem("u_done")
        ulo_ready = sem("ulo_ready")
        usum_ready = sem("usum_ready")
        c_ready = sem("c_ready")
        v_ready = sem("v_ready")
        s_ready = sem("s_ready")
        y_ready = sem("y_ready")
        yhi_ready = sem("yhi_ready")
        ylo_ready = sem("ylo_ready")
        wo_done = sem("wo_done")
        x1_ready = sem("x1_ready")
        x1hi_ready = sem("x1hi_ready")
        x1lo_ready = sem("x1lo_ready")
        z_done = sem("z_done")
        h_ready = sem("h_ready")
        ht_done = sem("ht_done")
        hthi_ready = sem("hthi_ready")
        htlo_ready = sem("htlo_ready")
        out_ready = sem("out_ready")
        stored = [sem(f"stored{i}") for i in range(2)]

        def groups(engine, body):
            body(0, 0, True, False)
            body(1, 1, True, False)
            with engine.Fori(1, GROUPS // 2 - 1) as pair:
                body(2 * pair, 0, False, False)
                body(2 * pair + 1, 1, False, False)
            body(GROUPS - 2, 0, False, False)
            body(GROUPS - 1, 1, False, True)

        toeplitz = bass.AP(hankel.tensor, 0, [[1, P], [2 * P, D], [1, TIME]])
        block = ctx.enter_context(nc.Block())

        @block.sync
        def _(sp):
            sp.dma_start(bp_c[:, 0:1], bp.rearrange("(p o) -> p o", o=1)).then_inc(bp_loaded, DMA)

            def load_wp(c):
                rows = bass.ds(c * P, P)
                sp.dma_start(wp_now[:, 0:P], Wp[rows, :]).then_inc(wp_loaded, DMA)
                sp.dma_start(wp_now[:, P:P + 1], conv_b[rows].rearrange("(p o) -> p o", o=1)).then_inc(wp_loaded, DMA)

            load_wp(0)

            def load_ring(n, slot):
                sp.dma_start(t_ring[:, slot], toeplitz[:, bass.ds(n * CH, CH), :]).then_inc(ring_loaded[slot], DMA)
                sp.dma_start(x_ring[:, slot], x_rev[:, bass.ds(n * CH, CH), :]).then_inc(ring_loaded[slot], DMA)

            for n in range(RING):
                load_ring(n, n)
            per_chunk = P // CH
            with sp.Fori(0, KC - 1) as c:
                for q in range(per_chunk):
                    sp.wait_ge(conv_done, BANKS * c + 2 * (q + 1))
                    load_ring(per_chunk * c + q + RING, q % RING)
                    if q == per_chunk - 1:
                        sp.wait_ge(proj_done, BANKS * (c + 1))
                        load_wp(c + 1)
            for q in range(per_chunk - RING):
                sp.wait_ge(conv_done, BANKS * (KC - 1) + 2 * (q + 1))
                load_ring(per_chunk * (KC - 1) + q + RING, q % RING)

            sp.wait_ge(conv_done, BANKS * KC)
            sp.dma_start(w_f[:], Wx.rearrange("(c p) n -> p c n", p=P)).then_inc(wx_loaded, DMA)

            def load_x(g, slot):
                sp.dma_start(x_f[:, slot], x_dtb[:, bass.ds(g * G, G), :].rearrange("(c p) t b -> p c t b", p=P))\
                  .then_inc(x_loaded[slot], DMA)

            load_x(0, 0)
            load_x(1, 1)
            sp.dma_start(bias_f[0:1, :], b.rearrange("(o n) -> o n", o=1)).then_inc(late_loaded, DMA)
            sp.dma_start(bias_f[32:33, :], b.rearrange("(o n) -> o n", o=1)).then_inc(late_loaded, DMA)
            sp.dma_start(h0_f[:], h0_t.rearrange("(c p) b -> p c b", p=P)).then_inc(late_loaded, DMA)
            sp.wait_ge(weights_ready, 4)
            sp.dma_start(w_f[:], Wh.rearrange("(c p) n -> p c n", p=P)).then_inc(wh_loaded, DMA)

            def stores_and_loads(g, par, first, last):
                if not (last or (isinstance(g, int) and g == GROUPS - 2)):
                    sp.wait_ge(x1_ready, KC * (g + 1))
                    load_x(g + 2, par)
                sp.wait_ge(out_ready, G * (g + 1))
                sp.dma_start(out[:, bass.ds(g * G, G), :].rearrange("(c p) t b -> p c t b", p=P), x1_f[:, par])\
                  .then_inc(stored[par], DMA)

            groups(sp, stores_and_loads)
            for par in range(2):
                sp.wait_ge(stored[par], DMA * GROUPS // 2)

        @block.gpsimd
        def _(pool):
            nc.gpsimd.memset(ident[:], 0.0).then_inc(ident_zero, 1)
            pool.wait_ge(ident_zero, 1)
            nc.gpsimd.affine_select(out=ident[:], in_=ident[:], compare_op=ALU.not_equal, fill=1.0, base=0,
                                    pattern=[[-1, P]], channel_multiplier=1).then_inc(ident_ready, 1)
            pool.wait_ge(small_loaded, 9 * DMA)
            nc.gpsimd.tensor_copy(ws_hl[:, :, 0:N], ws_f[:]).then_inc(pool_step, 1)
            pool.wait_ge(wo_scaled, 1)
            nc.gpsimd.tensor_copy(wo_hi[:], wo_f[:]).then_inc(pool_step, 1)
            pool.wait_ge(pool_step, 2)
            nc.gpsimd.tensor_tensor(ws_hl[:, :, N:2 * N], ws_f[:], f(ws_hl[:, :, 0:N]), ALU.subtract)\
              .then_inc(weights_ready, 1)
            nc.gpsimd.tensor_tensor(wo_lo[:], wo_f[:], f(wo_hi[:]), ALU.subtract).then_inc(weights_ready, 1)
            pool.wait_ge(conv_done, BANKS * KC)
            nc.gpsimd.memset(f(ones[:]), 1.0).then_inc(weights_ready, 1)
            nc.gpsimd.memset(f(bias_hl[:]), 0.0).then_inc(pool_step, 1)
            pool.wait_ge(wx_loaded, DMA)
            nc.gpsimd.tensor_copy(wx_hi[:], w_f[:]).then_inc(pool_step, 1)
            pool.wait_ge(pool_step, 4)
            nc.gpsimd.tensor_tensor(wx_lo[:], w_f[:], f(wx_hi[:]), ALU.subtract).then_inc(weights_ready, 1)
            pool.wait_ge(late_loaded, 3 * DMA)
            pool.wait_ge(weights_ready, 4)
            nc.gpsimd.tensor_copy(bias_hl[0:1, :], bias_f[0:1, :]).then_inc(pool_step, 1)
            pool.wait_ge(pool_step, 5)
            nc.gpsimd.tensor_copy(bias_hl[32:33, :], bias_f[32:33, :]).then_inc(pool_step, 1)
            pool.wait_ge(pool_step, 6)
            nc.gpsimd.tensor_tensor(bias_f[32:33, :], bias_f[32:33, :], f(bias_hl[32:33, :]), ALU.subtract)\
              .then_inc(pool_step, 1)
            pool.wait_ge(pool_step, 7)
            nc.gpsimd.tensor_copy(bias_hl[32:33, :], bias_f[32:33, :]).then_inc(weights_ready, 1)
            pool.wait_ge(weights_ready, 5)
            pool.wait_ge(wh_loaded, DMA)
            nc.gpsimd.tensor_copy(wh_hi[:], w_f[:]).then_inc(pool_step, 1)
            pool.wait_ge(pool_step, 8)
            nc.gpsimd.tensor_tensor(wh_lo[:], w_f[:], f(wh_hi[:]), ALU.subtract).then_inc(weights_ready, 1)

            def x1_rest(g, par):
                for c in range(KC):
                    pool.wait_ge(x1hi_ready, KC * g + c + 1)
                    nc.gpsimd.tensor_tensor(x1_lo[:, c], x1_f[:, par, c], f(x1_hi[:, c]), ALU.subtract)\
                      .then_inc(x1lo_ready, 1)

            x1_rest(0, 0)
            with pool.Fori(0, GROUPS // 2 - 1) as pair:
                x1_rest(2 * pair + 1, 1)
                x1_rest(2 * pair + 2, 0)
            x1_rest(GROUPS - 1, 1)

        @block.scalar
        def _(act):
            act.dma_start(bo_c[:], bo).then_inc(small_loaded, DMA)
            act.dma_start(bs_c[:, 0:1], bs.rearrange("(p o) -> p o", o=1)).then_inc(small_loaded, DMA)
            for half in (0, N):
                act.dma_start(rates[half:half + N, 0:1], A_log.rearrange("(p o) -> p o", o=1)).then_inc(small_loaded, DMA)
                act.dma_start(rates[half:half + N, 1:2], dt_log.rearrange("(p o) -> p o", o=1)).then_inc(small_loaded, DMA)
                act.dma_start(wo_f[half:half + N, :], Wo).then_inc(small_loaded, DMA)
            act.dma_start(ws_f[:], Ws.rearrange("(c p) n -> p c n", p=P)).then_inc(small_loaded, DMA)

            nc.scalar.preload_act_table_set("natural_log_exp_and_others")
            act.wait_ge(rate_step, 1)
            nc.scalar.activation(rates_e[:], rates[:, 2:4], ACT.Exp, scale=-1.0).then_inc(rate_act, 1)
            act.wait_ge(rate_act, 1)
            nc.scalar.activation(rates[:, 4:6], rates_e[:], ACT.Ln, bias=1.0).then_inc(rate_act, 1)

            with act.Fori(0, KC) as c:
                with act.Fori(0, BANKS // 4) as i:
                    m = 4 * i
                    for k in (0, 2):
                        act.wait_ge(conv_done, BANKS * c + m + k + 1)
                        nc.scalar.copy(conv[:, :, bass.ds((m + k) * PER_BANK, PER_BANK)],
                                       CONV[k][:].rearrange("p (d l) -> p l d", d=PER_BANK)).then_inc(conv_copied_act, 1)
                act.wait_ge(wp_loaded, 2 * DMA * (c + 1))
                with act.Fori(0, BANKS // 2) as i:
                    m = 2 * i
                    for k in range(2):
                        act.wait_ge(turn_done, BANKS * c + m + k + 1)
                        nc.scalar.activation(turned[:, k], TURN[k][:], ACT.Identity, bias=wp_now[:, P:P + 1])\
                          .then_inc(turn_copied, 1)

            def split_x(g, par):
                act.wait_ge(x_loaded[par], DMA * ((g - par) // 2 + 1) if isinstance(g, int) else (g - par) * (DMA // 2) + DMA)
                wait(act, u_done, g)
                nc.scalar.copy(x_hi[:], x_f[:, par]).then_inc(xhi_ready, 1)

            nc.scalar.preload_act_table_set("natural_log_exp_and_others")
            for i in range(SOFT):
                act.wait_ge(abs_ready, i + 1)
                nc.scalar.activation(soft[i % 2], soft[i % 2], ACT.Exp, scale=-1.0).then_inc(exp_ready, 1)
                act.wait_ge(exp_ready, i + 1)
                nc.scalar.activation(soft[i % 2], soft[i % 2], ACT.Ln, bias=1.0).then_inc(ln_ready, 1)

            def u_copy(g):
                act.wait_ge(u_done, g + 1)
                nc.scalar.copy(u_lo[:], UB[N:P, :]).then_inc(ulo_ready, 1)
                cols = bass.ds(g * (G * BATCH), G * BATCH)
                nc.scalar.activation(bc[N:P, cols], bc[N:P, cols], ACT.Tanh).then_inc(c_ready, 1)

            def y_copy(g):
                act.wait_ge(y_ready, g + 1)
                wait(act, wo_done, KC * g)
                nc.scalar.copy(y_hl[N:P, :], y_f[N:P, :]).then_inc(yhi_ready, 1)

            def x1_copy(g, par):
                for c in range(KC):
                    act.wait_ge(x1_ready, KC * g + c + 1)
                    nc.scalar.copy(x1_hi[:, c], x1_f[:, par, c]).then_inc(x1hi_ready, 1)

            split_x(0, 0)
            act.wait_ge(late_loaded, 3 * DMA)
            nc.scalar.copy(hT_hi[:], h0_f[:]).then_inc(hthi_ready, 1)
            u_copy(0)
            y_copy(0)
            split_x(1, 1)
            x1_copy(0, 0)

            def steps(g, par, first, last):
                for s in range(G):
                    t = g * G + s
                    act.wait_ge(z_done, t + 1)
                    nc.scalar.activation(h_f[:], ZB[s % 2][:], ACT.Tanh).then_inc(h_ready, 1)
                    act.wait_ge(ht_done, t + 1)
                    nc.scalar.copy(hT_hi[:], HB[s % 2][:].rearrange("p (c b) -> p c b", c=KC)).then_inc(hthi_ready, 1)
                    if last:
                        continue
                    if s == 0:
                        u_copy(g + 1)
                    if s == 1:
                        y_copy(g + 1)
                    if s == 2:
                        x1_copy(g + 1, 1 - par)
                    if s == 3 and not (isinstance(g, int) and g == GROUPS - 2):
                        split_x(g + 2, par)

            groups(act, steps)

        @block.vector
        def _(dve):
            dve.wait_ge(small_loaded, 9 * DMA)
            nc.vector.scalar_tensor_tensor(out=rates[:, 2:4], in0=rates[:, 0:2], scalar=-1.0, in1=rates[:, 0:2],
                                           op0=ALU.mult, op1=ALU.max).then_inc(rate_step, 1)
            dve.wait_ge(rate_act, 2)
            nc.vector.scalar_tensor_tensor(out=rates_e[:], in0=rates[:, 0:2], scalar=0.0, in1=rates[:, 4:6],
                                           op0=ALU.max, op1=ALU.add).then_inc(rate_step, 1)
            dve.wait_ge(rate_step, 2)
            nc.vector.tensor_tensor(rates[:, 4:5], rates_e[:, 0:1], rates_e[:, 1:2], ALU.mult).then_inc(rate_step, 1)
            nc.vector.tensor_scalar(wo_f[:], wo_f[:], rates_e[:, 1:2], None, ALU.mult).then_inc(wo_scaled, 1)
            dve.wait_ge(rate_step, 3)
            nc.vector.tensor_scalar(rates[:, 5:6], rates[:, 4:5], -1.0, 1.0, ALU.mult, ALU.add).then_inc(rate_step, 1)
            decay = rates[N:P, 5:6]
            dve.wait_ge(bp_loaded, DMA)
            nc.vector.tensor_copy(bc[:], bp_c[:, 0:1].to_broadcast([P, TIME * BATCH]))

            with dve.Fori(0, KC) as c:
                with dve.Fori(0, BANKS // 4) as i:
                    m = 4 * i
                    for k in (1, 3):
                        dve.wait_ge(conv_done, BANKS * c + m + k + 1)
                        nc.vector.tensor_copy(conv[:, :, bass.ds((m + k) * PER_BANK, PER_BANK)],
                                              CONV[k][:].rearrange("p (d l) -> p l d", d=PER_BANK))\
                          .then_inc(conv_copied_dve, 1)
                with dve.Fori(0, BANKS // 2) as i:
                    m = 2 * i
                    for k in range(2):
                        dve.wait_ge(proj_done, BANKS * c + m + k + 1)
                        cols = bass.ds((m + k) * 512, 512)
                        nc.vector.tensor_tensor(bc[:, cols], PROJ[k][:], bc[:, cols], ALU.add).then_inc(proj_added, 1)

            dve.wait_ge(proj_added, BANKS * KC)

            def soft_abs(i):
                v = bc[0:N, i * PIECE:(i + 1) * PIECE]
                nc.vector.scalar_tensor_tensor(out=soft[i % 2], in0=v, scalar=-1.0, in1=v, op0=ALU.mult, op1=ALU.max)\
                  .then_inc(abs_ready, 1)

            soft_abs(0)
            soft_abs(1)
            for i in range(SOFT):
                dve.wait_ge(ln_ready, i + 1)
                v = bc[0:N, i * PIECE:(i + 1) * PIECE]
                nc.vector.scalar_tensor_tensor(out=v, in0=v, scalar=0.0, in1=soft[i % 2],
                                               op0=ALU.max, op1=ALU.add).then_inc(b_ready, 1)
                if i + 2 < SOFT:
                    dve.wait_ge(b_ready, i + 1)
                    soft_abs(i + 2)

            def split_x(g, par):
                dve.wait_ge(xhi_ready, g + 1)
                nc.vector.tensor_tensor(x_lo[:], x_f[:, par], f(x_hi[:]), ALU.subtract).then_inc(xlo_ready, 1)

            def u_to_state(g):
                dve.wait_ge(ulo_ready, g + 1)
                nc.vector.scalar_tensor_tensor(out=u_sum[:], in0=UB[0:N, :], scalar=bs_c[:, 0:1], in1=u_lo[:],
                                               op0=ALU.add, op1=ALU.add).then_inc(usum_ready, 1)
                dve.wait_ge(usum_ready, g + 1)
                cols = bass.ds(g * (G * BATCH), G * BATCH)
                nc.vector.tensor_tensor(v_f[N:P].rearrange("p t b -> p (t b)"), u_sum[:], bc[0:N, cols], ALU.mult)\
                  .then_inc(v_ready, 1)
                dve.wait_ge(v_ready, g + 1)
                for s in range(G):
                    if not (isinstance(g, int) and g == 0 and s == 0):
                        dve.wait_ge(s_ready, G * g + s)
                        nc.vector.scalar_tensor_tensor(out=s_f[N:P, s], in0=s_f[N:P, (s - 1) % G], scalar=decay,
                                                       in1=v_f[N:P, s], op0=ALU.mult, op1=ALU.add).then_inc(s_ready, 1)
                    else:
                        nc.vector.tensor_copy(s_f[N:P, 0], v_f[N:P, 0]).then_inc(s_ready, 1)

            def state_to_y(g):
                dve.wait_ge(s_ready, G * (g + 1))
                dve.wait_ge(c_ready, g + 1)
                cols = bass.ds(g * (G * BATCH), G * BATCH)
                nc.vector.tensor_tensor(y_f[N:P, :], s_f[N:P].rearrange("p t b -> p (t b)"), bc[N:P, cols], ALU.mult)\
                  .then_inc(y_ready, 1)
                dve.wait_ge(yhi_ready, g + 1)
                nc.vector.tensor_tensor(y_hl[0:N, :], y_f[N:P, :], f(y_hl[N:P, :]), ALU.subtract).then_inc(ylo_ready, 1)

            def x1_sum(g, par):
                if isinstance(g, int):
                    wait(dve, stored[par], DMA * ((g - par) // 2))
                else:
                    dve.wait_ge(stored[par], (g - par) * (DMA // 2))
                for c in range(KC):
                    dve.wait_ge(wo_done, KC * g + c + 1)
                    nc.vector.scalar_tensor_tensor(out=x1_f[:, par, c].rearrange("p t b -> p (t b)"), in0=XB[c % 2][:],
                                                   scalar=bo_c[:, c:c + 1],
                                                   in1=x_f[:, par, c].rearrange("p t b -> p (t b)"),
                                                   op0=ALU.add, op1=ALU.add).then_inc(x1_ready, 1)

            split_x(0, 0)
            dve.wait_ge(hthi_ready, 1)
            nc.vector.tensor_tensor(hT_lo[:], h0_f[:], f(hT_hi[:]), ALU.subtract).then_inc(htlo_ready, 1)
            u_to_state(0)
            state_to_y(0)
            split_x(1, 1)
            x1_sum(0, 0)

            def steps(g, par, first, last):
                for s in range(G):
                    t = g * G + s
                    turned_h = HB[s % 2][:].rearrange("p (c b) -> p c b", c=KC)
                    dve.wait_ge(hthi_ready, t + 2)
                    nc.vector.tensor_tensor(hT_lo[:], turned_h, f(hT_hi[:]), ALU.subtract).then_inc(htlo_ready, 1)
                    nc.vector.tensor_tensor(x1_f[:, par, :, s, :], turned_h, x1_f[:, par, :, s, :], ALU.add)\
                      .then_inc(out_ready, 1)
                    if last:
                        continue
                    if s == 0:
                        u_to_state(g + 1)
                    if s == 1:
                        state_to_y(g + 1)
                    if s == 2:
                        x1_sum(g + 1, 1 - par)
                    if s == 3 and not (isinstance(g, int) and g == GROUPS - 2):
                        split_x(g + 2, par)

            groups(dve, steps)

        @block.tensor
        def _(pe):
            pe.wait_ge(ident_ready, 1)
            with pe.Fori(0, KC) as c:
                for d in range(P):
                    slot, m = (d // CH) % RING, d // PER_BANK
                    if d % CH == 0:
                        pe.wait_ge(ring_loaded[slot], 2 * DMA * (P // CH // RING) * c + 2 * DMA * (d // CH // RING + 1))
                    if d % PER_BANK == 0 and m >= 4:
                        if m % 2 == 0:
                            pe.wait_ge(conv_copied_act, BANKS // 2 * c + (m - 4) // 2 + 1)
                        else:
                            pe.wait_ge(conv_copied_dve, BANKS // 2 * c + (m - 4) // 2 + 1)
                    mm = nc.tensor.matmul(CONV[m % 4][:, bass.ts(d % PER_BANK, TIME)], x_ring[:, slot, d % CH],
                                          t_ring[:, slot, d % CH], start=True, stop=True)
                    if d % PER_BANK == PER_BANK - 1:
                        mm.then_inc(conv_done, 1)
                pe.wait_ge(conv_copied_act, BANKS // 2 * (c + 1))
                pe.wait_ge(conv_copied_dve, BANKS // 2 * (c + 1))
                pe.wait_ge(wp_loaded, 2 * DMA * (c + 1))
                for m in range(BANKS + 1):
                    if m < BANKS:
                        if m == 0:
                            pass
                        for i in range(PER_BANK):
                            mm = nc.tensor.transpose(TURN[m % 2][:, bass.ts(i, P)], conv[:, m * PER_BANK + i], ident[:])
                        mm.then_inc(turn_done, 1)
                    if m > 0:
                        pe.wait_ge(turn_copied, BANKS * c + m)
                        if m > 2:
                            pe.wait_ge(proj_added, BANKS * c + m - 2)
                        nc.tensor.matmul(PROJ[(m - 1) % 2][:], wp_now[:, 0:P], turned[:, (m - 1) % 2], start=True, stop=True)\
                          .then_inc(proj_done, 1)

            def u_product(g):
                pe.wait_ge(xhi_ready, g + 1)
                wait(pe, usum_ready, g)
                for k in range(KC):
                    nc.tensor.matmul(UB[:], ws_hl[:, k], x_hi[:, k], start=(k == 0), stop=False)
                pe.wait_ge(xlo_ready, g + 1)
                for k in range(KC):
                    mm = nc.tensor.matmul(UB[:], ws_hl[:, k], x_lo[:, k], start=False, stop=(k == KC - 1))
                mm.then_inc(u_done, 1)

            def wo_product(g):
                pe.wait_ge(yhi_ready, g + 1)
                pe.wait_ge(ylo_ready, g + 1)
                for c in range(KC):
                    wait(pe, x1_ready, KC * g + c - 1)
                    nc.tensor.matmul(XB[c % 2][:], wo_hi[:, bass.ts(c, P)], y_hl[:], start=True, stop=False)
                    nc.tensor.matmul(XB[c % 2][:], wo_lo[:, bass.ts(c, P)], y_hl[:], start=False, stop=True)\
                      .then_inc(wo_done, 1)

            def z_first(g, par, s):
                if s == 0:
                    pe.wait_ge(x1hi_ready, KC * (g + 1))
                z = ZB[s % 2][:]
                nc.tensor.matmul(z, ones[:], bias_hl[:], start=True, stop=False)
                for k in range(KC):
                    nc.tensor.matmul(z, x1_hi[:, k, s], wx_hi[:, k], start=False, stop=False)

            def z_second(g, par, s):
                z = ZB[s % 2][:]
                for k in range(KC):
                    nc.tensor.matmul(z, x1_hi[:, k, s], wx_lo[:, k], start=False, stop=False)
                if s == 0:
                    pe.wait_ge(x1lo_ready, KC * (g + 1))
                for k in range(KC):
                    nc.tensor.matmul(z, x1_lo[:, k, s], wx_hi[:, k], start=False, stop=False)

            def z_recur(t, s):
                z = ZB[s % 2][:]
                pe.wait_ge(hthi_ready, t + 1)
                for k in range(KC):
                    nc.tensor.matmul(z, hT_hi[:, k], wh_hi[:, k], start=False, stop=False)
                    nc.tensor.matmul(z, hT_hi[:, k], wh_lo[:, k], start=False, stop=False)
                pe.wait_ge(htlo_ready, t + 1)
                for k in range(KC):
                    mm = nc.tensor.matmul(z, hT_lo[:, k], wh_hi[:, k], start=False, stop=(k == KC - 1))
                mm.then_inc(z_done, 1)

            pe.wait_ge(weights_ready, 2)
            u_product(0)
            pe.wait_ge(b_ready, SOFT)
            wo_product(0)
            pe.wait_ge(weights_ready, 6)
            z_first(0, 0, 0)
            z_second(0, 0, 0)
            z_recur(0, 0)

            def steps(g, par, first, last):
                for s in range(G):
                    t = g * G + s
                    end = last and s == G - 1
                    ahead = (g, par, s + 1) if s < G - 1 else (g + 1, 1 - par, 0)
                    if not end:
                        z_first(*ahead)
                    pe.wait_ge(h_ready, t + 1)
                    for k in range(KC):
                        mm = nc.tensor.transpose(HB[s % 2][:, bass.ts(k, P)], h_f[:, bass.ts(k, P)], ident[:])
                    mm.then_inc(ht_done, 1)
                    if end:
                        continue
                    z_second(*ahead)
                    if not last:
                        if s == 0:
                            u_product(g + 1)
                        if s == 2:
                            wo_product(g + 1)
                    z_recur(t + 1, (s + 1) % G)

            groups(pe, steps)


def kernel(**inputs):
    import numpy as np
    import concourse.bacc as bacc
    from concourse.bass_utils import run_bass_kernel_spmd

    x = np.asarray(inputs["x"])
    cond = np.asarray(inputs["cond_1024"])
    zeros = np.zeros((D, TIME - 1), cond.dtype)
    arrays = {
        "x_rev": x.transpose(1, 2, 0)[::-1],
        "x_dtb": x.transpose(2, 1, 0),
        "hankel": np.concatenate([zeros, cond[::-1].T, zeros[:, :1]], axis=1),
        "h0_t": cond.T,
        "conv_b": inputs["L0_cond_conv_b"],
        "Wp": inputs["L0_cond_Wp"],
        "bp": inputs["L0_cond_bp"],
        "Ws": inputs["L0_cond_Ws"],
        "bs": inputs["L0_cond_bs"],
        "A_log": inputs["L0_cond_A_log"],
        "dt_log": inputs["L0_cond_dt_log"],
        "Wo": inputs["L0_cond_Wo"],
        "bo": np.asarray(inputs["L0_cond_bo"]).reshape(KC, P).T,
        "Wx": inputs["L1_cond_Wx"],
        "Wh": inputs["L1_cond_Wh"],
        "b": inputs["L1_cond_b"],
    }
    arrays = {name: np.ascontiguousarray(a) for name, a in arrays.items()}
    nc = bacc.Bacc("TRN2", target_bir_lowering=False, num_devices=1)
    args = {
        name: nc.dram_tensor(name, a.shape, mybir.dt.from_np(a.dtype), kind="ExternalInput").ap()
        for name, a in arrays.items()
    }
    out = nc.dram_tensor("out", (D, TIME, BATCH), F32, kind="ExternalOutput").ap()
    build(nc, **args, out=out)
    result = run_bass_kernel_spmd(nc, [arrays], core_ids=[0])
    return result.results[0]["out"].transpose(2, 1, 0)
```

```python
from contextlib import ExitStack

import concourse.bass as bass
from concourse import mybir

F32 = mybir.dt.float32
F32R = mybir.dt.float32r
U32 = mybir.dt.uint32
ALU = mybir.AluOpType
ACT = mybir.ActivationFunctionType

BATCH = 128
TIME = 128
D = 512
N = 64
P = 128
KC = D // P
RING = 16
CH = 4
PER_BANK = 4
LOADS = D // CH
BANKS = P // PER_BANK
G = 4
GROUPS = TIME // G
EXP_LAG = 5
SOFT_SLOTS = 4
LAG = 3
DMA = 16


def wait(engine, sem, value):
    if not isinstance(value, int) or value > 0:
        engine.wait_ge(sem, value)


def build(nc, x_rev, x_dtb, hankel, h0_t, conv_b, Wp, bp, Ws, bs, A_log, dt_log, Wo, bo, Wx, Wh, b, out):
    ctx = ExitStack()
    with ctx:
        def sb(stack, name, shape, dt=F32):
            return stack.enter_context(nc.sbuf_tensor(name, shape, dt))

        def sem(name):
            return ctx.enter_context(nc.semaphore(name))

        bank = [ctx.enter_context(nc.psum_tensor(f"bank{i}", [P, 512], F32)) for i in range(8)]
        CONV, TURN, PROJ = bank[0:4], bank[4:6] + bank[0:2], bank[2:4] + bank[6:8]
        ZB, HB, XB, UB = bank[0:2], bank[2:4], bank[6:8] + bank[4:6], bank[5]

        bc = sb(ctx, "bc", [P, TIME * BATCH])
        ident = sb(ctx, "ident", [P, P])
        wp_now = sb(ctx, "wp_now", [P, P + 1])
        turned = sb(ctx, "turned", [P, 4, 512])
        ws_f = turned[:, 2, 0:KC * N].rearrange("p (c n) -> p c n", c=KC)
        wo_f = turned[:, 3]
        bp_c = sb(ctx, "bp_c", [P, 1])
        bo_c = sb(ctx, "bo_c", [P, KC])
        bs_c = sb(ctx, "bs_c", [N, 1])
        rates = sb(ctx, "rates", [P, 6])
        rates_e = sb(ctx, "rates_e", [P, 2])
        ws_hl = sb(ctx, "ws_hl", [P, KC, 2 * N], F32R)
        wo_hi = sb(ctx, "wo_hi", [P, D], F32R)
        wo_lo = sb(ctx, "wo_lo", [P, D], F32R)

        with ExitStack() as first:
            t_ring = sb(first, "t_ring", [P, RING, CH, TIME])
            x_ring = sb(first, "x_ring", [P, RING, CH, BATCH])
            conv = sb(first, "conv", [P, TIME, P])
        wx_hi = sb(ctx, "wx_hi", [P, KC, D], F32R)
        wx_lo = sb(ctx, "wx_lo", [P, KC, D], F32R)
        wh_hi = sb(ctx, "wh_hi", [P, KC, D], F32R)
        wh_lo = sb(ctx, "wh_lo", [P, KC, D], F32R)
        with ExitStack() as splitting:
            w_f = sb(splitting, "w_f", [P, KC, D])
        x_hi = sb(ctx, "x_hi", [P, KC, G, BATCH], F32R)
        hT_hi = sb(ctx, "hT_hi", [P, KC, BATCH], F32R)
        hT_lo = sb(ctx, "hT_lo", [P, KC, BATCH], F32R)
        b_rows = sb(ctx, "b_rows", [P, D])
        h0_f = sb(ctx, "h0_f", [P, KC, BATCH])
        x_f = sb(ctx, "x_f", [P, 2, KC, G, BATCH])
        x_lo = sb(ctx, "x_lo", [P, KC, G, BATCH], F32R)
        x1_f = sb(ctx, "x1_f", [P, 2, KC, G, BATCH])
        x1_hi = sb(ctx, "x1_hi", [P, KC, G, BATCH], F32R)
        x1_lo = sb(ctx, "x1_lo", [P, KC, G, BATCH], F32R)
        h_f = sb(ctx, "h_f", [P, D])
        z_f = sb(ctx, "z_f", [P, D])
        u_lo = sb(ctx, "u_lo", [N, G * BATCH])
        u_sum = sb(ctx, "u_sum", [N, G * BATCH])
        v_f = sb(ctx, "v_f", [P, G, BATCH])
        s_f = sb(ctx, "s_f", [P, G, BATCH])
        y_f = sb(ctx, "y_f", [P, G * BATCH])
        y_hl = sb(ctx, "y_hl", [P, G * BATCH], F32R)

        soft = [x_f[0:N, 1, i].rearrange("p t b -> p (t b)") for i in range(SOFT_SLOTS)]

        def f(ap):
            return ap.bitcast(F32)

        ring_loaded = [sem(f"ring_loaded{i}") for i in range(RING)]
        conv_done = sem("conv_done")
        conv_copied_act = sem("conv_copied_act")
        conv_copied_dve = sem("conv_copied_dve")
        turn_done = sem("turn_done")
        turn_copied = sem("turn_copied")
        wp_loaded = sem("wp_loaded")
        proj_done = sem("proj_done")
        proj_added = sem("proj_added")
        ident_zero = sem("ident_zero")
        ident_ready = sem("ident_ready")
        bp_loaded = sem("bp_loaded")
        small_loaded = sem("small_loaded")
        rate_step = sem("rate_step")
        rate_act = sem("rate_act")
        wo_scaled = sem("wo_scaled")
        wx_loaded = sem("wx_loaded")
        wh_loaded = sem("wh_loaded")
        late_loaded = sem("late_loaded")
        pool_step = sem("pool_step")
        weights_ready = sem("weights_ready")
        abs_ready = sem("abs_ready")
        exp_ready = sem("exp_ready")
        ln_ready = sem("ln_ready")
        b_ready = sem("b_ready")
        x_loaded = [sem(f"x_loaded{i}") for i in range(2)]
        xhi_ready = sem("xhi_ready")
        xlo_ready = sem("xlo_ready")
        u_done = sem("u_done")
        ulo_ready = sem("ulo_ready")
        usum_ready = sem("usum_ready")
        c_ready = sem("c_ready")
        v_ready = sem("v_ready")
        s_ready = sem("s_ready")
        y_ready = sem("y_ready")
        yhi_ready = sem("yhi_ready")
        ylo_ready = sem("ylo_ready")
        wo_done = sem("wo_done")
        x1_ready = sem("x1_ready")
        x1hi_ready = sem("x1hi_ready")
        x1lo_ready = sem("x1lo_ready")
        z_done = sem("z_done")
        zsum_ready = sem("zsum_ready")
        h_ready = sem("h_ready")
        ht_done = sem("ht_done")
        hthi_ready = sem("hthi_ready")
        htlo_ready = sem("htlo_ready")
        out_ready = sem("out_ready")
        stored = [sem(f"stored{i}") for i in range(2)]

        def groups(engine, body):
            body(0, 0, True, False)
            body(1, 1, True, False)
            with engine.Fori(1, GROUPS // 2 - 1) as pair:
                body(2 * pair, 0, False, False)
                body(2 * pair + 1, 1, False, False)
            body(GROUPS - 2, 0, False, False)
            body(GROUPS - 1, 1, False, True)

        toeplitz = bass.AP(hankel.tensor, 0, [[1, P], [2 * P, D], [1, TIME]])
        block = ctx.enter_context(nc.Block())

        @block.sync
        def _(sp):
            def load_wp(c):
                rows = bass.ds(c * P, P)
                sp.dma_start(wp_now[:, 0:P], Wp[rows, :]).then_inc(wp_loaded, DMA)
                sp.dma_start(wp_now[:, P:P + 1], conv_b[rows].rearrange("(p o) -> p o", o=1)).then_inc(wp_loaded, DMA)

            def load_ring(n, slot):
                sp.dma_start(t_ring[:, slot], toeplitz[:, bass.ds(n * CH, CH), :]).then_inc(ring_loaded[slot], DMA)
                sp.dma_start(x_ring[:, slot], x_rev[:, bass.ds(n * CH, CH), :]).then_inc(ring_loaded[slot], DMA)

            for n in range(RING):
                load_ring(n, n)
                if n == 0:
                    load_wp(0)
                    sp.dma_start(bp_c[:, 0:1], bp.rearrange("(p o) -> p o", o=1)).then_inc(bp_loaded, DMA)
            per_chunk = P // CH
            with sp.Fori(0, KC - 1) as c:
                for q in range(per_chunk):
                    sp.wait_ge(conv_done, BANKS * c + CH // PER_BANK * (q + 1))
                    load_ring(per_chunk * c + q + RING, q % RING)
                    if q == per_chunk - 1:
                        sp.wait_ge(proj_done, BANKS * (c + 1))
                        load_wp(c + 1)
            for q in range(per_chunk - RING):
                sp.wait_ge(conv_done, BANKS * (KC - 1) + CH // PER_BANK * (q + 1))
                load_ring(per_chunk * (KC - 1) + q + RING, q % RING)

            sp.wait_ge(conv_done, BANKS * KC)
            sp.dma_start(w_f[:], Wx.rearrange("(c p) n -> p c n", p=P)).then_inc(wx_loaded, DMA)

            def load_x(g, slot):
                sp.dma_start(x_f[:, slot], x_dtb[:, bass.ds(g * G, G), :].rearrange("(c p) t b -> p c t b", p=P))\
                  .then_inc(x_loaded[slot], DMA)

            load_x(0, 0)
            sp.dma_start(b_rows[:], b.partition_broadcast(P)).then_inc(late_loaded, DMA)
            sp.dma_start(h0_f[:], h0_t.rearrange("(c p) b -> p c b", p=P)).then_inc(late_loaded, DMA)
            sp.wait_ge(weights_ready, 3)
            sp.dma_start(w_f[:], Wh.rearrange("(c p) n -> p c n", p=P)).then_inc(wh_loaded, DMA)
            sp.wait_ge(b_ready, BANKS)
            load_x(1, 1)

            def stores_and_loads(g, par, first, last):
                if not (last or (isinstance(g, int) and g == GROUPS - 2)):
                    sp.wait_ge(x1_ready, KC * (g + 1))
                    load_x(g + 2, par)
                sp.wait_ge(out_ready, G * (g + 1))
                sp.dma_start(out[:, bass.ds(g * G, G), :].rearrange("(c p) t b -> p c t b", p=P), x1_f[:, par])\
                  .then_inc(stored[par], DMA)

            groups(sp, stores_and_loads)
            for par in range(2):
                sp.wait_ge(stored[par], DMA * GROUPS // 2)

        @block.gpsimd
        def _(pool):
            nc.gpsimd.memset(ident[:], 0.0).then_inc(ident_zero, 1)
            pool.wait_ge(ident_zero, 1)
            nc.gpsimd.affine_select(out=ident[:], in_=ident[:], compare_op=ALU.not_equal, fill=1.0, base=0,
                                    pattern=[[-1, P]], channel_multiplier=1).then_inc(ident_ready, 1)
            pool.wait_ge(small_loaded, 9 * DMA)
            nc.gpsimd.tensor_copy(ws_hl[:, :, 0:N], ws_f).then_inc(pool_step, 1)
            pool.wait_ge(wo_scaled, 1)
            nc.gpsimd.tensor_copy(wo_hi[:], wo_f).then_inc(pool_step, 1)
            pool.wait_ge(pool_step, 2)
            nc.gpsimd.tensor_tensor(ws_hl[:, :, N:2 * N], ws_f, f(ws_hl[:, :, 0:N]), ALU.subtract)\
              .then_inc(weights_ready, 1)
            nc.gpsimd.tensor_tensor(wo_lo[:], wo_f, f(wo_hi[:]), ALU.subtract).then_inc(weights_ready, 1)
            pool.wait_ge(conv_done, BANKS * KC)
            pool.wait_ge(wx_loaded, DMA)
            nc.gpsimd.tensor_copy(wx_hi[:], w_f[:]).then_inc(pool_step, 1)
            pool.wait_ge(pool_step, 3)
            nc.gpsimd.tensor_tensor(wx_lo[:], w_f[:], f(wx_hi[:]), ALU.subtract).then_inc(weights_ready, 1)
            pool.wait_ge(wh_loaded, DMA)
            nc.gpsimd.tensor_copy(wh_hi[:], w_f[:]).then_inc(pool_step, 1)
            pool.wait_ge(pool_step, 4)
            nc.gpsimd.tensor_tensor(wh_lo[:], w_f[:], f(wh_hi[:]), ALU.subtract).then_inc(weights_ready, 1)

            pool.wait_ge(late_loaded, 2 * DMA)
            nc.gpsimd.tensor_copy(hT_hi[:], h0_f[:]).then_inc(hthi_ready, 1)
            pool.wait_ge(weights_ready, 4)
            pool.wait_ge(x_loaded[0], DMA)
            nc.gpsimd.tensor_copy(x_hi[:], x_f[:, 0]).then_inc(xhi_ready, 1)
            pool.wait_ge(hthi_ready, 1)
            nc.gpsimd.tensor_tensor(hT_lo[:], h0_f[:], f(hT_hi[:]), ALU.subtract).then_inc(htlo_ready, 1)
            pool.wait_ge(turn_done, BANKS * KC)

            def x_rest(g, par):
                pool.wait_ge(xhi_ready, g + 1)
                nc.gpsimd.tensor_tensor(x_lo[:], x_f[:, par], f(x_hi[:]), ALU.subtract).then_inc(xlo_ready, 1)

            def x1_rest(g, par, chunks=range(KC)):
                for c in chunks:
                    pool.wait_ge(x1hi_ready, KC * g + c + 1)
                    nc.gpsimd.tensor_tensor(x1_lo[:, c], x1_f[:, par, c], f(x1_hi[:, c]), ALU.subtract)\
                      .then_inc(x1lo_ready, 1)

            x_rest(0, 0)
            x1_rest(0, 0, range(KC // 2, KC))
            x_rest(1, 1)
            with pool.Fori(0, GROUPS // 2 - 1) as pair:
                for g, par in ((2 * pair + 1, 1), (2 * pair + 2, 0)):
                    x_rest(g + 1, 1 - par)
                    x1_rest(g, par)
            x1_rest(GROUPS - 1, 1)

        @block.scalar
        def _(act):
            act.dma_start(bo_c[:], bo).then_inc(small_loaded, DMA)
            act.dma_start(bs_c[:, 0:1], bs.rearrange("(p o) -> p o", o=1)).then_inc(small_loaded, DMA)
            for half in (0, N):
                act.dma_start(rates[half:half + N, 0:1], A_log.rearrange("(p o) -> p o", o=1)).then_inc(small_loaded, DMA)
                act.dma_start(rates[half:half + N, 1:2], dt_log.rearrange("(p o) -> p o", o=1)).then_inc(small_loaded, DMA)
                act.dma_start(wo_f[half:half + N, :], Wo).then_inc(small_loaded, DMA)
            act.dma_start(ws_f, Ws.rearrange("(c p) n -> p c n", p=P)).then_inc(small_loaded, DMA)

            nc.scalar.preload_act_table_set("natural_log_exp_and_others")
            act.wait_ge(rate_step, 1)
            nc.scalar.activation(rates_e[:], rates[:, 2:4], ACT.Exp).then_inc(rate_act, 1)
            act.wait_ge(rate_act, 1)
            nc.scalar.activation(rates[:, 4:6], rates_e[:], ACT.Ln, bias=1.0).then_inc(rate_act, 1)

            def copy_conv(c):
                with act.Fori(0, BANKS // 4) as i:
                    m = 4 * i
                    for k in (0, 2):
                        act.wait_ge(conv_done, BANKS * c + m + k + 1)
                        nc.scalar.copy(conv[:, :, bass.ds((m + k) * PER_BANK, PER_BANK)],
                                       CONV[k][:].rearrange("p (d l) -> p l d", d=PER_BANK)).then_inc(conv_copied_act, 1)
                act.wait_ge(wp_loaded, 2 * DMA * (c + 1))

            def copy_turned(c, m, k):
                act.wait_ge(turn_done, BANKS * c + m + k + 1)
                nc.scalar.activation(turned[:, k], TURN[k][:], ACT.Identity, bias=wp_now[:, P:P + 1])\
                  .then_inc(turn_copied, 1)

            act.wait_ge(weights_ready, 2)
            with act.Fori(0, KC - 1) as c:
                copy_conv(c)
                with act.Fori(0, BANKS // 4) as i:
                    for k in range(4):
                        copy_turned(c, 4 * i, k)

            nc.scalar.preload_act_table_set("natural_log_exp_and_others")
            copy_conv(KC - 1)

            def soft_exp(n, k):
                act.wait_ge(abs_ready, n + 1)
                nc.scalar.activation(soft[k], soft[k], ACT.Exp, scale=-1.0).then_inc(exp_ready, 1)

            def soft_ln(n, k):
                act.wait_ge(exp_ready, n + 1)
                nc.scalar.activation(soft[k], soft[k], ACT.Ln, bias=1.0).then_inc(ln_ready, 1)

            def soft_banks(m, k):
                if not isinstance(m, int) or EXP_LAG <= m < BANKS + EXP_LAG:
                    soft_exp(m - EXP_LAG, (k - EXP_LAG) % SOFT_SLOTS)
                if not isinstance(m, int) or EXP_LAG < m:
                    soft_ln(m - EXP_LAG - 1, (k - EXP_LAG - 1) % SOFT_SLOTS)

            for m in range(8):
                copy_turned(KC - 1, m - m % 4, m % 4)
                soft_banks(m, m % 4)
            with act.Fori(2, BANKS // 4) as i:
                for k in range(4):
                    copy_turned(KC - 1, 4 * i, k)
                    soft_banks(4 * i + k, k)
            for m in range(BANKS, BANKS + EXP_LAG + 1):
                soft_banks(m, m % 4)

            def split_x(g, par):
                act.wait_ge(x_loaded[par], DMA * ((g - par) // 2 + 1) if isinstance(g, int) else (g - par) * (DMA // 2) + DMA)
                wait(act, u_done, g)
                nc.scalar.copy(x_hi[:], x_f[:, par]).then_inc(xhi_ready, 1)

            def u_copy(g):
                act.wait_ge(u_done, g + 1)
                nc.scalar.copy(u_lo[:], UB[N:P, :]).then_inc(ulo_ready, 1)
                cols = bass.ds(g * (G * BATCH), G * BATCH)
                nc.scalar.activation(bc[N:P, cols], bc[N:P, cols], ACT.Tanh).then_inc(c_ready, 1)

            def y_copy(g):
                act.wait_ge(y_ready, g + 1)
                wait(act, wo_done, KC * g)
                nc.scalar.copy(y_hl[N:P, :], y_f[N:P, :]).then_inc(yhi_ready, 1)

            def x1_copy(g, par):
                for c in range(KC):
                    act.wait_ge(x1_ready, KC * g + c + 1)
                    nc.scalar.copy(x1_hi[:, c], x1_f[:, par, c]).then_inc(x1hi_ready, 1)

            u_copy(0)
            y_copy(0)
            x1_copy(0, 0)
            split_x(1, 1)

            def steps(g, par, first, last):
                for s in range(G):
                    t = g * G + s
                    act.wait_ge(zsum_ready, t + 1)
                    nc.scalar.activation(h_f[:], z_f[:], ACT.Tanh).then_inc(h_ready, 1)
                    if s == 2 and not last:
                        y_copy(g + 1)
                    act.wait_ge(ht_done, t + 1)
                    nc.scalar.copy(hT_hi[:], HB[s % 2][:].rearrange("p (c b) -> p c b", c=KC)).then_inc(hthi_ready, 1)
                    if last:
                        continue
                    if s == 0:
                        u_copy(g + 1)
                    if s == 2:
                        x1_copy(g + 1, 1 - par)
                    if s == 1 and not (isinstance(g, int) and g == GROUPS - 2):
                        split_x(g + 2, par)

            groups(act, steps)

        @block.vector
        def _(dve):
            dve.wait_ge(small_loaded, 9 * DMA)
            nc.vector.scalar_tensor_tensor(out=rates[:, 2:4], in0=rates[:, 0:2], scalar=-1.0, in1=rates[:, 0:2],
                                           op0=ALU.mult, op1=ALU.min).then_inc(rate_step, 1)
            dve.wait_ge(rate_act, 2)
            nc.vector.scalar_tensor_tensor(out=rates_e[:], in0=rates[:, 0:2], scalar=0.0, in1=rates[:, 4:6],
                                           op0=ALU.max, op1=ALU.add).then_inc(rate_step, 1)
            dve.wait_ge(rate_step, 2)
            nc.vector.tensor_tensor(rates[:, 4:5], rates_e[:, 0:1], rates_e[:, 1:2], ALU.mult).then_inc(rate_step, 1)
            nc.vector.tensor_scalar(wo_f, wo_f, rates_e[:, 1:2], None, ALU.mult).then_inc(wo_scaled, 1)
            dve.wait_ge(rate_step, 3)
            nc.vector.tensor_scalar(rates[:, 5:6], rates[:, 4:5], -1.0, 1.0, ALU.mult, ALU.add).then_inc(rate_step, 1)
            decay = rates[N:P, 5:6]
            dve.wait_ge(bp_loaded, DMA)
            nc.vector.tensor_copy(bc[:], bp_c[:, 0:1].to_broadcast([P, TIME * BATCH]))

            def copy_conv(c):
                with dve.Fori(0, BANKS // 4) as i:
                    m = 4 * i
                    for k in (1, 3):
                        dve.wait_ge(conv_done, BANKS * c + m + k + 1)
                        nc.vector.tensor_copy(conv[:, :, bass.ds((m + k) * PER_BANK, PER_BANK)],
                                              CONV[k][:].rearrange("p (d l) -> p l d", d=PER_BANK))\
                          .then_inc(conv_copied_dve, 1)

            def add_proj(c, m, k):
                dve.wait_ge(proj_done, BANKS * c + m + k + 1)
                cols = bass.ds((m + k) * 512, 512)
                nc.vector.tensor_tensor(bc[:, cols], PROJ[k][:], bc[:, cols], ALU.add).then_inc(proj_added, 1)

            with dve.Fori(0, KC - 1) as c:
                copy_conv(c)
                with dve.Fori(0, BANKS // 4) as i:
                    for k in range(4):
                        add_proj(c, 4 * i, k)

            copy_conv(KC - 1)

            def soft_abs(n, k):
                v = bc[0:N, bass.ds(n * 512, 512)]
                dve.wait_ge(proj_added, BANKS * (KC - 1) + n + 1)
                nc.vector.tensor_scalar(soft[k].bitcast(U32), v.bitcast(U32), 0x7fffffff, None, ALU.bitwise_and)\
                  .then_inc(abs_ready, 1)

            def soft_sum(n, k):
                dve.wait_ge(ln_ready, n + 1)
                v = bc[0:N, bass.ds(n * 512, 512)]
                nc.vector.scalar_tensor_tensor(out=v, in0=v, scalar=0.0, in1=soft[k], op0=ALU.max, op1=ALU.add)\
                  .then_inc(b_ready, 1)

            for k in range(4):
                add_proj(KC - 1, 0, k)
                soft_abs(k, k)
                if k == 3:
                    soft_sum(0, 0)
            with dve.Fori(1, BANKS // 4) as i:
                for k in range(4):
                    add_proj(KC - 1, 4 * i, k)
                    soft_abs(4 * i + k, k)
                    soft_sum(4 * i + k - 3, (k - 3) % SOFT_SLOTS)
            for n in range(BANKS - 3, BANKS):
                soft_sum(n, n % SOFT_SLOTS)

            def u_to_v(g):
                dve.wait_ge(ulo_ready, g + 1)
                nc.vector.scalar_tensor_tensor(out=u_sum[:], in0=UB[0:N, :], scalar=bs_c[:, 0:1], in1=u_lo[:],
                                               op0=ALU.add, op1=ALU.add).then_inc(usum_ready, 1)
                dve.wait_ge(usum_ready, g + 1)
                cols = bass.ds(g * (G * BATCH), G * BATCH)
                nc.vector.tensor_tensor(v_f[N:P].rearrange("p t b -> p (t b)"), u_sum[:], bc[0:N, cols], ALU.mult)\
                  .then_inc(v_ready, 1)
                dve.wait_ge(v_ready, g + 1)

            def state(g, s):
                if isinstance(g, int) and g == 0 and s == 0:
                    nc.vector.tensor_copy(s_f[N:P, 0], v_f[N:P, 0]).then_inc(s_ready, 1)
                else:
                    dve.wait_ge(s_ready, G * g + s)
                    nc.vector.scalar_tensor_tensor(out=s_f[N:P, s], in0=s_f[N:P, (s - 1) % G], scalar=decay,
                                                   in1=v_f[N:P, s], op0=ALU.mult, op1=ALU.add).then_inc(s_ready, 1)

            def state_to_y(g):
                dve.wait_ge(s_ready, G * (g + 1))
                dve.wait_ge(c_ready, g + 1)
                cols = bass.ds(g * (G * BATCH), G * BATCH)
                nc.vector.tensor_tensor(y_f[N:P, :], s_f[N:P].rearrange("p t b -> p (t b)"), bc[N:P, cols], ALU.mult)\
                  .then_inc(y_ready, 1)

            def y_rest(g):
                dve.wait_ge(yhi_ready, g + 1)
                nc.vector.tensor_tensor(y_hl[0:N, :], y_f[N:P, :], f(y_hl[N:P, :]), ALU.subtract).then_inc(ylo_ready, 1)

            def x1_sum(g, par, chunks):
                if 0 in chunks:
                    if isinstance(g, int):
                        wait(dve, stored[par], DMA * ((g - par) // 2))
                    else:
                        dve.wait_ge(stored[par], (g - par) * (DMA // 2))
                for c in chunks:
                    dve.wait_ge(wo_done, KC * g + c + 1)
                    nc.vector.scalar_tensor_tensor(out=x1_f[:, par, c].rearrange("p t b -> p (t b)"), in0=XB[c][:],
                                                   scalar=bo_c[:, c:c + 1],
                                                   in1=x_f[:, par, c].rearrange("p t b -> p (t b)"),
                                                   op0=ALU.add, op1=ALU.add).then_inc(x1_ready, 1)

            u_to_v(0)
            for s in range(G):
                state(0, s)
            state_to_y(0)
            y_rest(0)
            x1_sum(0, 0, range(KC))
            for c in range(KC // 2):
                dve.wait_ge(x1hi_ready, c + 1)
                nc.vector.tensor_tensor(x1_lo[:, c], x1_f[:, 0, c], f(x1_hi[:, c]), ALU.subtract).then_inc(x1lo_ready, 1)

            def steps(g, par, first, last):
                for s in range(G):
                    t = g * G + s
                    turned_h = HB[s % 2][:].rearrange("p (c b) -> p c b", c=KC)
                    dve.wait_ge(z_done, t + 1)
                    nc.vector.tensor_tensor(z_f[:], ZB[s % 2][:], b_rows[:], ALU.add).then_inc(zsum_ready, 1)
                    if s == 2 and not last:
                        y_rest(g + 1)
                    dve.wait_ge(hthi_ready, t + 2)
                    nc.vector.tensor_tensor(hT_lo[:], turned_h, f(hT_hi[:]), ALU.subtract).then_inc(htlo_ready, 1)
                    if s == 2 and not last:
                        x1_sum(g + 1, 1 - par, range(0, 2))
                    nc.vector.tensor_tensor(x1_f[:, par, :, s, :], turned_h, x1_f[:, par, :, s, :], ALU.add)\
                      .then_inc(out_ready, 1)
                    if last:
                        continue
                    if s == 0:
                        u_to_v(g + 1)
                        state(g + 1, 0)
                        state(g + 1, 1)
                    if s == 1:
                        state(g + 1, 2)
                        state(g + 1, 3)
                        state_to_y(g + 1)
                    if s == 2:
                        x1_sum(g + 1, 1 - par, range(2, KC))

            groups(dve, steps)

        @block.tensor
        def _(pe):
            pe.wait_ge(ident_ready, 1)
            with pe.Fori(0, KC) as c:
                for d in range(P):
                    slot, m = (d // CH) % RING, d // PER_BANK
                    if d % CH == 0:
                        pe.wait_ge(ring_loaded[slot], 2 * DMA * (P // CH // RING) * c + 2 * DMA * (d // CH // RING + 1))
                    if d % PER_BANK == 0 and m >= 4:
                        if m % 2 == 0:
                            pe.wait_ge(conv_copied_act, BANKS // 2 * c + (m - 4) // 2 + 1)
                        else:
                            pe.wait_ge(conv_copied_dve, BANKS // 2 * c + (m - 4) // 2 + 1)
                    mm = nc.tensor.matmul(CONV[m % 4][:, bass.ts(d % PER_BANK, TIME)], x_ring[:, slot, d % CH],
                                          t_ring[:, slot, d % CH], start=True, stop=True)
                    if d % PER_BANK == PER_BANK - 1:
                        mm.then_inc(conv_done, 1)
                pe.wait_ge(conv_copied_act, BANKS // 2 * (c + 1))
                pe.wait_ge(conv_copied_dve, BANKS // 2 * (c + 1))
                pe.wait_ge(wp_loaded, 2 * DMA * (c + 1))
                for m in range(BANKS + LAG):
                    if m < BANKS:
                        for i in range(PER_BANK):
                            mm = nc.tensor.transpose(TURN[m % 4][:, bass.ts(i, P)], conv[:, m * PER_BANK + i], ident[:])
                        mm.then_inc(turn_done, 1)
                    if m >= LAG:
                        n = m - LAG
                        pe.wait_ge(turn_copied, BANKS * c + n + 1)
                        if n >= 4:
                            pe.wait_ge(proj_added, BANKS * c + n - 3)
                        nc.tensor.matmul(PROJ[n % 4][:], wp_now[:, 0:P], turned[:, n % 4], start=True, stop=True)\
                          .then_inc(proj_done, 1)
                pe.wait_ge(proj_added, BANKS * (c + 1) - 2)

            def u_first(g):
                pe.wait_ge(xhi_ready, g + 1)
                wait(pe, x1_ready, KC * g)
                for k in range(KC):
                    nc.tensor.matmul(UB[:], ws_hl[:, k], x_hi[:, k], start=(k == 0), stop=False)

            def u_second(g):
                pe.wait_ge(xlo_ready, g + 1)
                for k in range(KC):
                    mm = nc.tensor.matmul(UB[:], ws_hl[:, k], x_lo[:, k], start=False, stop=(k == KC - 1))
                mm.then_inc(u_done, 1)

            def wo_product(g):
                pe.wait_ge(yhi_ready, g + 1)
                pe.wait_ge(ylo_ready, g + 1)
                for c in range(KC):
                    nc.tensor.matmul(XB[c][:], wo_hi[:, bass.ts(c, P)], y_hl[:], start=True, stop=False)
                    nc.tensor.matmul(XB[c][:], wo_lo[:, bass.ts(c, P)], y_hl[:], start=False, stop=True)\
                      .then_inc(wo_done, 1)

            def z_first(s):
                z = ZB[s % 2][:]
                for k in range(KC):
                    nc.tensor.matmul(z, x1_hi[:, k, s], wx_hi[:, k], start=(k == 0), stop=False)
                    nc.tensor.matmul(z, x1_hi[:, k, s], wx_lo[:, k], start=False, stop=False)

            def z_second(s, stop=False):
                z = ZB[s % 2][:]
                for k in range(KC):
                    mm = nc.tensor.matmul(z, x1_lo[:, k, s], wx_hi[:, k], start=False, stop=stop and k == KC - 1)
                return mm

            def z_recur(t, s, stop=True):
                z = ZB[s % 2][:]
                pe.wait_ge(hthi_ready, t + 1)
                for k in range(KC):
                    nc.tensor.matmul(z, hT_hi[:, k], wh_hi[:, k], start=False, stop=False)
                    nc.tensor.matmul(z, hT_hi[:, k], wh_lo[:, k], start=False, stop=False)
                pe.wait_ge(htlo_ready, t + 1)
                for k in range(KC):
                    mm = nc.tensor.matmul(z, hT_lo[:, k], wh_hi[:, k], start=False, stop=stop and k == KC - 1)
                return mm

            pe.wait_ge(weights_ready, 2)
            u_first(0)
            u_second(0)
            wo_product(0)
            u_first(1)
            pe.wait_ge(weights_ready, 4)
            pe.wait_ge(x1hi_ready, KC)
            z_first(0)
            z_recur(0, 0, stop=False)
            pe.wait_ge(x1lo_ready, KC)
            z_second(0, stop=True).then_inc(z_done, 1)

            def steps(g, par, first, last):
                for s in range(G):
                    t = g * G + s
                    end = last and s == G - 1
                    ahead = (s + 1) % G
                    if not end:
                        if ahead == 0:
                            pe.wait_ge(x1hi_ready, KC * (g + 2))
                        z_first(ahead)
                    pe.wait_ge(h_ready, t + 1)
                    for k in range(KC):
                        mm = nc.tensor.transpose(HB[s % 2][:, bass.ts(k, P)], h_f[:, bass.ts(k, P)], ident[:])
                    mm.then_inc(ht_done, 1)
                    if end:
                        continue
                    if s == 0 and not last:
                        u_second(g + 1)
                    if s == 3 and not (isinstance(g, int) and g == GROUPS - 2):
                        u_first(g + 2)
                    if ahead == 0:
                        pe.wait_ge(x1lo_ready, KC * (g + 2))
                    z_second(ahead)
                    if s == 2 and not last:
                        wo_product(g + 1)
                    z_recur(t + 1, ahead).then_inc(z_done, 1)

            groups(pe, steps)


def kernel(**inputs):
    import numpy as np
    import concourse.bacc as bacc
    from concourse.bass_utils import run_bass_kernel_spmd

    x = np.asarray(inputs["x"])
    cond = np.asarray(inputs["cond_1024"])
    zeros = np.zeros((D, TIME - 1), cond.dtype)
    arrays = {
        "x_rev": x.transpose(1, 2, 0)[::-1],
        "x_dtb": x.transpose(2, 1, 0),
        "hankel": np.concatenate([zeros, cond[::-1].T, zeros[:, :1]], axis=1),
        "h0_t": cond.T,
        "conv_b": inputs["L0_cond_conv_b"],
        "Wp": inputs["L0_cond_Wp"],
        "bp": inputs["L0_cond_bp"],
        "Ws": inputs["L0_cond_Ws"],
        "bs": inputs["L0_cond_bs"],
        "A_log": inputs["L0_cond_A_log"],
        "dt_log": inputs["L0_cond_dt_log"],
        "Wo": inputs["L0_cond_Wo"],
        "bo": np.asarray(inputs["L0_cond_bo"]).reshape(KC, P).T,
        "Wx": inputs["L1_cond_Wx"],
        "Wh": inputs["L1_cond_Wh"],
        "b": inputs["L1_cond_b"],
    }
    arrays = {name: np.ascontiguousarray(a) for name, a in arrays.items()}
    nc = bacc.Bacc("TRN2", target_bir_lowering=False, num_devices=1)
    args = {
        name: nc.dram_tensor(name, a.shape, mybir.dt.from_np(a.dtype), kind="ExternalInput").ap()
        for name, a in arrays.items()
    }
    out = nc.dram_tensor("out", (D, TIME, BATCH), F32, kind="ExternalOutput").ap()
    build(nc, **args, out=out)
    result = run_bass_kernel_spmd(nc, [arrays], core_ids=[0])
    return result.results[0]["out"].transpose(2, 1, 0)
```

```python
from contextlib import ExitStack

import concourse.bass as bass
from concourse import mybir

F32 = mybir.dt.float32
F32R = mybir.dt.float32r
U32 = mybir.dt.uint32
ALU = mybir.AluOpType
ACT = mybir.ActivationFunctionType

BATCH = 128
TIME = 128
D = 512
N = 64
P = 128
KC = D // P
RING = 16
CH = 4
PER_BANK = 4
LOADS = D // CH
BANKS = P // PER_BANK
G = 4
GROUPS = TIME // G
SOFT_SLOTS = 4
VECTORS = KC + 5
PAIRS = BANKS // 2
LAG = 3
DMA = 16


def wait(engine, sem, value):
    if not isinstance(value, int) or value > 0:
        engine.wait_ge(sem, value)


def build(nc, x_rev, x_dtb, hankel, h0_t, vectors, Wp, Ws, Wo, Wx, Wh, b, out):
    ctx = ExitStack()
    with ctx:
        def sb(stack, name, shape, dt=F32):
            return stack.enter_context(nc.sbuf_tensor(name, shape, dt))

        def sem(name):
            return ctx.enter_context(nc.semaphore(name))

        bank = [ctx.enter_context(nc.psum_tensor(f"bank{i}", [P, 512], F32)) for i in range(8)]
        CONV, TURN, PROJ = bank[0:4], bank[4:6] + bank[0:2], bank[2:4] + bank[6:8]
        ZB, HB, XB, UB = bank[0:2], bank[2:4], bank[6:8] + bank[4:6], bank[5]

        bc = sb(ctx, "bc", [P, TIME * BATCH])
        ident = sb(ctx, "ident", [P, P])
        wp_now = sb(ctx, "wp_now", [P, 2 * P + 1])
        turned = sb(ctx, "turned", [P, 4, 512])
        ws_f = turned[:, 2, 0:KC * N].rearrange("p (c n) -> p c n", c=KC)
        wo_f = turned[:, 3]
        vec = sb(ctx, "vec", [P, VECTORS])
        bo_c, bp_c, bs_c, logs = vec[:, 0:KC], vec[:, KC:KC + 2], vec[0:N, KC + 2:KC + 3], vec[:, KC + 3:KC + 5]
        rates = sb(ctx, "rates", [P, 4])
        rates_e = sb(ctx, "rates_e", [P, 2])
        ws_hl = sb(ctx, "ws_hl", [P, KC, 2 * N], F32R)
        wo_hi = sb(ctx, "wo_hi", [P, D], F32R)
        wo_lo = sb(ctx, "wo_lo", [P, D], F32R)

        with ExitStack() as first:
            t_ring = sb(first, "t_ring", [P, RING, CH, TIME])
            x_ring = sb(first, "x_ring", [P, RING, CH, BATCH])
            conv = sb(first, "conv", [P, TIME, P])
        wx_hi = sb(ctx, "wx_hi", [P, KC, D], F32R)
        wx_lo = sb(ctx, "wx_lo", [P, KC, D], F32R)
        wh_hi = sb(ctx, "wh_hi", [P, KC, D], F32R)
        wh_lo = sb(ctx, "wh_lo", [P, KC, D], F32R)
        with ExitStack() as splitting:
            w_f = sb(splitting, "w_f", [P, KC, D])
        x_hi = sb(ctx, "x_hi", [P, KC, G, BATCH], F32R)
        hT_hi = sb(ctx, "hT_hi", [P, KC, BATCH], F32R)
        hT_lo = sb(ctx, "hT_lo", [P, KC, BATCH], F32R)
        b_rows = sb(ctx, "b_rows", [P, D])
        h0_f = sb(ctx, "h0_f", [P, KC, BATCH])
        x_f = sb(ctx, "x_f", [P, 2, KC, G, BATCH])
        x_lo = sb(ctx, "x_lo", [P, KC, G, BATCH], F32R)
        x1_f = sb(ctx, "x1_f", [P, 2, KC, G, BATCH])
        x1_hi = sb(ctx, "x1_hi", [P, KC, G, BATCH], F32R)
        x1_lo = sb(ctx, "x1_lo", [P, KC, G, BATCH], F32R)
        h_f = sb(ctx, "h_f", [P, D])
        z_f = sb(ctx, "z_f", [P, D])
        u_lo = sb(ctx, "u_lo", [N, G * BATCH])
        u_sum = sb(ctx, "u_sum", [P, G * BATCH])
        c_f = sb(ctx, "c_f", [P, G * BATCH])
        v_f = sb(ctx, "v_f", [P, G, BATCH])
        s_f = sb(ctx, "s_f", [P, G, BATCH])
        y_f = sb(ctx, "y_f", [P, G * BATCH])
        y_hl = sb(ctx, "y_hl", [P, G * BATCH], F32R)

        soft = [x_f[:, 1, i].rearrange("p t b -> p (t b)") for i in range(SOFT_SLOTS)]

        def rows_of_b(par):
            return slice(N, P) if par else slice(0, N)

        def rows_of_c(par):
            return rows_of_b(1 - par)

        def f(ap):
            return ap.bitcast(F32)

        ring_loaded = [sem(f"ring_loaded{i}") for i in range(RING)]
        conv_done = sem("conv_done")
        conv_copied_act = sem("conv_copied_act")
        conv_copied_dve = sem("conv_copied_dve")
        turn_done = sem("turn_done")
        turn_copied = sem("turn_copied")
        wp_loaded = sem("wp_loaded")
        proj_done = sem("proj_done")
        proj_added = sem("proj_added")
        ident_zero = sem("ident_zero")
        ident_ready = sem("ident_ready")
        vec_loaded = sem("vec_loaded")
        ws_wo_loaded = sem("ws_wo_loaded")
        rate_step = sem("rate_step")
        rate_act = sem("rate_act")
        wo_scaled = sem("wo_scaled")
        wx_loaded = sem("wx_loaded")
        wh_loaded = sem("wh_loaded")
        late_loaded = sem("late_loaded")
        pool_step = sem("pool_step")
        weights_ready = sem("weights_ready")
        abs_ready = sem("abs_ready")
        abs_odd_ready = sem("abs_odd_ready")
        exp_ready = sem("exp_ready")
        ln_ready = sem("ln_ready")
        max_ready = sem("max_ready")
        b_ready = sem("b_ready")
        last_b_ready = sem("last_b_ready")
        x_loaded = [sem(f"x_loaded{i}") for i in range(2)]
        xhi_ready = sem("xhi_ready")
        xlo_ready = sem("xlo_ready")
        u_done = sem("u_done")
        ulo_ready = sem("ulo_ready")
        usum_ready = sem("usum_ready")
        c_ready = sem("c_ready")
        v_ready = sem("v_ready")
        s_ready = sem("s_ready")
        y_ready = sem("y_ready")
        yhi_ready = sem("yhi_ready")
        ylo_ready = sem("ylo_ready")
        wo_done = sem("wo_done")
        x1_ready = sem("x1_ready")
        x1hi_ready = sem("x1hi_ready")
        x1lo_ready = sem("x1lo_ready")
        z_done = sem("z_done")
        zsum_ready = sem("zsum_ready")
        h_ready = sem("h_ready")
        ht_done = sem("ht_done")
        hthi_ready = sem("hthi_ready")
        htlo_ready = sem("htlo_ready")
        out_ready = sem("out_ready")
        stored = [sem(f"stored{i}") for i in range(2)]

        def groups(engine, body):
            body(0, 0, True, False)
            body(1, 1, True, False)
            with engine.Fori(1, GROUPS // 2 - 1) as pair:
                body(2 * pair, 0, False, False)
                body(2 * pair + 1, 1, False, False)
            body(GROUPS - 2, 0, False, False)
            body(GROUPS - 1, 1, False, True)

        toeplitz = bass.AP(hankel.tensor, 0, [[1, P], [2 * P, D], [1, TIME]])
        block = ctx.enter_context(nc.Block())

        @block.sync
        def _(sp):
            def load_wp(c):
                rows = bass.ds(c * P, P)
                sp.dma_start(wp_now[:], Wp[rows, :]).then_inc(wp_loaded, DMA)

            def load_ring(n, slot):
                sp.dma_start(t_ring[:, slot], toeplitz[:, bass.ds(n * CH, CH), :]).then_inc(ring_loaded[slot], DMA)
                sp.dma_start(x_ring[:, slot], x_rev[:, bass.ds(n * CH, CH), :]).then_inc(ring_loaded[slot], DMA)

            for n in range(RING):
                load_ring(n, n)
                if n == 0:
                    sp.dma_start(vec[:], vectors).then_inc(vec_loaded, DMA)
                    sp.dma_start(wo_f, Wo).then_inc(ws_wo_loaded, DMA)
                    sp.dma_start(ws_f, Ws.rearrange("(c p) n -> p c n", p=P)).then_inc(ws_wo_loaded, DMA)
            load_wp(0)
            per_chunk = P // CH
            with sp.Fori(0, KC - 1) as c:
                for q in range(per_chunk):
                    sp.wait_ge(conv_done, BANKS * c + CH // PER_BANK * (q + 1))
                    load_ring(per_chunk * c + q + RING, q % RING)
                    if q == per_chunk - 1:
                        sp.wait_ge(proj_done, BANKS * (c + 1))
                        load_wp(c + 1)
            for q in range(per_chunk - RING):
                sp.wait_ge(conv_done, BANKS * (KC - 1) + CH // PER_BANK * (q + 1))
                load_ring(per_chunk * (KC - 1) + q + RING, q % RING)

            sp.wait_ge(conv_done, BANKS * KC)
            sp.dma_start(w_f[:], Wx.rearrange("(c p) n -> p c n", p=P)).then_inc(wx_loaded, DMA)

            def load_x(g, slot):
                sp.dma_start(x_f[:, slot], x_dtb[:, bass.ds(g * G, G), :].rearrange("(c p) t b -> p c t b", p=P))\
                  .then_inc(x_loaded[slot], DMA)

            load_x(0, 0)
            sp.dma_start(b_rows[:], b.partition_broadcast(P)).then_inc(late_loaded, DMA)
            sp.dma_start(h0_f[:], h0_t.rearrange("(c p) b -> p c b", p=P)).then_inc(late_loaded, DMA)
            sp.wait_ge(weights_ready, 3)
            sp.dma_start(w_f[:], Wh.rearrange("(c p) n -> p c n", p=P)).then_inc(wh_loaded, DMA)
            sp.wait_ge(b_ready, BANKS - 2)
            sp.wait_ge(last_b_ready, 2)
            load_x(1, 1)

            def stores_and_loads(g, par, first, last):
                if not (last or (isinstance(g, int) and g == GROUPS - 2)):
                    sp.wait_ge(x1_ready, KC * (g + 1))
                    load_x(g + 2, par)
                sp.wait_ge(out_ready, G * (g + 1))
                sp.dma_start(out[:, bass.ds(g * G, G), :].rearrange("(c p) t b -> p c t b", p=P), x1_f[:, par])\
                  .then_inc(stored[par], DMA)

            groups(sp, stores_and_loads)
            for par in range(2):
                sp.wait_ge(stored[par], DMA * GROUPS // 2)

        @block.gpsimd
        def _(pool):
            nc.gpsimd.memset(ident[:], 0.0).then_inc(ident_zero, 1)
            pool.wait_ge(ident_zero, 1)
            nc.gpsimd.affine_select(out=ident[:], in_=ident[:], compare_op=ALU.not_equal, fill=1.0, base=0,
                                    pattern=[[-1, P]], channel_multiplier=1).then_inc(ident_ready, 1)
            pool.wait_ge(ws_wo_loaded, 2 * DMA)
            nc.gpsimd.tensor_copy(ws_hl[:, :, 0:N], ws_f).then_inc(pool_step, 1)
            pool.wait_ge(wo_scaled, 1)
            nc.gpsimd.tensor_copy(wo_hi[:], wo_f).then_inc(pool_step, 1)
            pool.wait_ge(pool_step, 2)
            nc.gpsimd.tensor_tensor(ws_hl[:, :, N:2 * N], ws_f, f(ws_hl[:, :, 0:N]), ALU.subtract)\
              .then_inc(weights_ready, 1)
            nc.gpsimd.tensor_tensor(wo_lo[:], wo_f, f(wo_hi[:]), ALU.subtract).then_inc(weights_ready, 1)
            pool.wait_ge(conv_done, BANKS * KC)
            pool.wait_ge(wx_loaded, DMA)
            nc.gpsimd.tensor_copy(wx_hi[:], w_f[:]).then_inc(pool_step, 1)
            pool.wait_ge(pool_step, 3)
            nc.gpsimd.tensor_tensor(wx_lo[:], w_f[:], f(wx_hi[:]), ALU.subtract).then_inc(weights_ready, 1)
            pool.wait_ge(wh_loaded, DMA)
            nc.gpsimd.tensor_copy(wh_hi[:], w_f[:]).then_inc(pool_step, 1)
            pool.wait_ge(pool_step, 4)
            nc.gpsimd.tensor_tensor(wh_lo[:], w_f[:], f(wh_hi[:]), ALU.subtract).then_inc(weights_ready, 1)

            pool.wait_ge(late_loaded, 2 * DMA)
            nc.gpsimd.tensor_copy(hT_hi[:], h0_f[:]).then_inc(hthi_ready, 1)
            pool.wait_ge(weights_ready, 4)
            pool.wait_ge(x_loaded[0], DMA)
            nc.gpsimd.tensor_copy(x_hi[:], x_f[:, 0]).then_inc(xhi_ready, 1)
            pool.wait_ge(hthi_ready, 1)
            nc.gpsimd.tensor_tensor(hT_lo[:], h0_f[:], f(hT_hi[:]), ALU.subtract).then_inc(htlo_ready, 1)
            pool.wait_ge(turn_done, BANKS * KC)

            def soft_max(q, par):
                pool.wait_ge(abs_odd_ready if par else abs_ready, q + 1)
                pool.wait_ge(max_ready if par else xlo_ready, 1)
                v = bc[rows_of_b(par), bass.ds((2 * q + par) * 512, 512)]
                nc.gpsimd.tensor_scalar(v, v, 0.0, None, ALU.max).then_inc(max_ready, 1)

            def soft_sum(q, par, slot):
                pool.wait_ge(ln_ready, q + 1)
                pool.wait_ge(max_ready, 2)
                wait(pool, last_b_ready, par)
                v = bc[rows_of_b(par), bass.ds((2 * q + par) * 512, 512)]
                nc.gpsimd.tensor_tensor(v, v, slot[rows_of_b(par), :], ALU.add).then_inc(last_b_ready, 1)

            def x_rest(g, par):
                pool.wait_ge(xhi_ready, g + 1)
                nc.gpsimd.tensor_tensor(x_lo[:], x_f[:, par], f(x_hi[:]), ALU.subtract).then_inc(xlo_ready, 1)

            def x1_rest(g, par, chunks=range(KC)):
                for c in chunks:
                    pool.wait_ge(x1hi_ready, KC * g + c + 1)
                    nc.gpsimd.tensor_tensor(x1_lo[:, c], x1_f[:, par, c], f(x1_hi[:, c]), ALU.subtract)\
                      .then_inc(x1lo_ready, 1)

            x_rest(0, 0)
            for par in range(2):
                soft_max(PAIRS - 1, par)
            for par in range(2):
                soft_sum(PAIRS - 1, par, soft[(PAIRS - 1) % 4])
            pool.wait_ge(last_b_ready, 2)
            x1_rest(0, 0, range(KC // 2, KC))
            x_rest(1, 1)
            with pool.Fori(0, GROUPS // 2 - 1) as pair:
                for g, par in ((2 * pair + 1, 1), (2 * pair + 2, 0)):
                    x_rest(g + 1, 1 - par)
                    x1_rest(g, par)
            x1_rest(GROUPS - 1, 1)

        @block.scalar
        def _(act):
            nc.scalar.preload_act_table_set("natural_log_exp_and_others")
            act.wait_ge(rate_step, 1)
            nc.scalar.activation(rates_e[:], rates[:, 0:2], ACT.Exp).then_inc(rate_act, 1)
            act.wait_ge(rate_act, 1)
            nc.scalar.activation(rates[:, 2:4], rates_e[:], ACT.Ln, bias=1.0).then_inc(rate_act, 1)

            def copy_conv(c):
                with act.Fori(0, BANKS // 4) as i:
                    m = 4 * i
                    for k in (0, 2):
                        act.wait_ge(conv_done, BANKS * c + m + k + 1)
                        nc.scalar.copy(conv[:, :, bass.ds((m + k) * PER_BANK, PER_BANK)],
                                       CONV[k][:].rearrange("p (d l) -> p l d", d=PER_BANK)).then_inc(conv_copied_act, 1)
                act.wait_ge(wp_loaded, DMA * (c + 1))

            def copy_turned(c, m, k):
                act.wait_ge(turn_done, BANKS * c + m + k + 1)
                nc.scalar.activation(turned[:, k], TURN[k][:], ACT.Identity, bias=wp_now[:, 2 * P:2 * P + 1])\
                  .then_inc(turn_copied, 1)

            act.wait_ge(weights_ready, 2)
            with act.Fori(0, KC - 1) as c:
                copy_conv(c)
                with act.Fori(0, BANKS // 4) as i:
                    for k in range(4):
                        copy_turned(c, 4 * i, k)

            nc.scalar.preload_act_table_set("natural_log_exp_and_others")
            copy_conv(KC - 1)

            def u_copy(g):
                act.wait_ge(u_done, g + 1)
                nc.scalar.copy(u_lo[:], UB[N:P, :]).then_inc(ulo_ready, 1)

            def tanh_c(g, par):
                wait(act, y_ready, g)
                cols = bass.ds(g * (G * BATCH), G * BATCH)
                nc.scalar.activation(c_f[N:P, :], bc[rows_of_c(par), cols], ACT.Tanh).then_inc(c_ready, 1)

            def soft_abs_odd(q, slot):
                n = 2 * q + 1
                act.wait_ge(proj_added, BANKS * (KC - 1) + n + 1)
                nc.scalar.activation(slot[N:P, :], bc[N:P, bass.ds(n * 512, 512)], ACT.Abs).then_inc(abs_odd_ready, 1)

            def soft_exp(q, slot):
                act.wait_ge(abs_ready, q + 1)
                act.wait_ge(abs_odd_ready, q + 1)
                nc.scalar.activation(slot, slot, ACT.Exp, scale=-1.0).then_inc(exp_ready, 1)

            def soft_ln(q, slot):
                act.wait_ge(exp_ready, q + 1)
                nc.scalar.activation(slot, slot, ACT.Ln, bias=1.0).then_inc(ln_ready, 1)

            def pair(q, i, soft_too):
                m = 2 * q - (2 * i) % 4
                copy_turned(KC - 1, m, (2 * i) % 4)
                if soft_too:
                    soft_exp(q - 3, soft[(i - 3) % 4])
                copy_turned(KC - 1, m, (2 * i) % 4 + 1)
                if soft_too:
                    soft_ln(q - 3, soft[(i - 3) % 4])
                    soft_abs_odd(q - 2, soft[(i - 2) % 4])

            for q in range(3):
                pair(q, q, False)
            soft_abs_odd(0, soft[0])
            pair(3, 3, True)
            with act.Fori(1, PAIRS // 4) as j:
                for i in range(4):
                    pair(4 * j + i, i, True)
            for q in range(PAIRS - 3, PAIRS):
                if q == PAIRS - 1:
                    u_copy(0)
                soft_exp(q, soft[q % 4])
                soft_ln(q, soft[q % 4])
                if q < PAIRS - 1:
                    soft_abs_odd(q + 1, soft[(q + 1) % 4])

            def split_x(g, par):
                act.wait_ge(x_loaded[par], DMA * ((g - par) // 2 + 1) if isinstance(g, int) else (g - par) * (DMA // 2) + DMA)
                wait(act, u_done, g)
                nc.scalar.copy(x_hi[:], x_f[:, par]).then_inc(xhi_ready, 1)

            def y_copy(g):
                act.wait_ge(y_ready, g + 1)
                wait(act, wo_done, KC * g)
                nc.scalar.copy(y_hl[N:P, :], y_f[N:P, :]).then_inc(yhi_ready, 1)

            def x1_copy(g, par):
                for c in range(KC):
                    act.wait_ge(x1_ready, KC * g + c + 1)
                    nc.scalar.copy(x1_hi[:, c], x1_f[:, par, c]).then_inc(x1hi_ready, 1)

            tanh_c(0, 0)
            y_copy(0)
            x1_copy(0, 0)
            split_x(1, 1)

            def steps(g, par, first, last):
                for s in range(G):
                    t = g * G + s
                    act.wait_ge(zsum_ready, t + 1)
                    nc.scalar.activation(h_f[:], z_f[:], ACT.Tanh).then_inc(h_ready, 1)
                    if s == 2 and not last:
                        y_copy(g + 1)
                    act.wait_ge(ht_done, t + 1)
                    nc.scalar.copy(hT_hi[:], HB[s % 2][:].rearrange("p (c b) -> p c b", c=KC)).then_inc(hthi_ready, 1)
                    if last:
                        continue
                    if s == 0:
                        u_copy(g + 1)
                        tanh_c(g + 1, 1 - par)
                    if s == 2:
                        x1_copy(g + 1, 1 - par)
                    if s == 1 and not (isinstance(g, int) and g == GROUPS - 2):
                        split_x(g + 2, par)

            groups(act, steps)

        @block.vector
        def _(dve):
            dve.wait_ge(vec_loaded, DMA)
            nc.vector.scalar_tensor_tensor(out=rates[:, 0:2], in0=logs, scalar=-1.0, in1=logs, op0=ALU.mult, op1=ALU.min)\
              .then_inc(rate_step, 1)
            dve.wait_ge(rate_act, 2)
            nc.vector.scalar_tensor_tensor(out=rates_e[:], in0=logs, scalar=0.0, in1=rates[:, 2:4], op0=ALU.max, op1=ALU.add)\
              .then_inc(rate_step, 1)
            dve.wait_ge(rate_step, 2)
            nc.vector.tensor_tensor(rates[:, 0:1], rates_e[:, 0:1], rates_e[:, 1:2], ALU.mult).then_inc(rate_step, 1)
            dve.wait_ge(ws_wo_loaded, 2 * DMA)
            nc.vector.tensor_scalar(wo_f, wo_f, rates_e[:, 1:2], None, ALU.mult).then_inc(wo_scaled, 1)
            dve.wait_ge(rate_step, 3)
            nc.vector.tensor_scalar(rates[:, 1:2], rates[:, 0:1], -1.0, 1.0, ALU.mult, ALU.add).then_inc(rate_step, 1)
            decay = rates[N:P, 1:2]
            for par in range(2):
                nc.vector.tensor_copy(bc[:].rearrange("p (g two c) -> p two g c", two=2, c=G * BATCH)[:, par],
                                      bp_c[:, par:par + 1].to_broadcast([P, GROUPS // 2, G * BATCH]))

            def copy_conv(c):
                with dve.Fori(0, BANKS // 4) as i:
                    m = 4 * i
                    for k in (1, 3):
                        dve.wait_ge(conv_done, BANKS * c + m + k + 1)
                        nc.vector.tensor_copy(conv[:, :, bass.ds((m + k) * PER_BANK, PER_BANK)],
                                              CONV[k][:].rearrange("p (d l) -> p l d", d=PER_BANK))\
                          .then_inc(conv_copied_dve, 1)

            def add_proj(c, m, k):
                dve.wait_ge(proj_done, BANKS * c + m + k + 1)
                cols = bass.ds((m + k) * 512, 512)
                nc.vector.tensor_tensor(bc[:, cols], PROJ[k][:], bc[:, cols], ALU.add).then_inc(proj_added, 1)

            with dve.Fori(0, KC - 1) as c:
                copy_conv(c)
                with dve.Fori(0, BANKS // 4) as i:
                    for k in range(4):
                        add_proj(c, 4 * i, k)

            copy_conv(KC - 1)

            def soft_abs_even(q, slot):
                n = 2 * q
                dve.wait_ge(proj_added, BANKS * (KC - 1) + n + 1)
                nc.vector.tensor_scalar(slot[0:N, :].bitcast(U32), bc[0:N, bass.ds(n * 512, 512)].bitcast(U32),
                                        0x7fffffff, None, ALU.bitwise_and).then_inc(abs_ready, 1)

            def soft_sum(q, par, slot):
                dve.wait_ge(ln_ready, q + 1)
                rows = rows_of_b(par)
                v = bc[rows, bass.ds((2 * q + par) * 512, 512)]
                nc.vector.scalar_tensor_tensor(out=v, in0=v, scalar=0.0, in1=slot[rows, :], op0=ALU.max, op1=ALU.add)\
                  .then_inc(b_ready, 1)

            def pair(q, i, soft_too):
                for par in range(2):
                    add_proj(KC - 1, 2 * q - (2 * i) % 4, (2 * i) % 4 + par)
                    if par == 0:
                        soft_abs_even(q, soft[i])
                    if soft_too:
                        soft_sum(q - 2, par, soft[(i - 2) % 4])

            for q in range(4):
                pair(q, q, q >= 2)
            with dve.Fori(1, PAIRS // 4) as j:
                for i in range(4):
                    pair(4 * j + i, i, True)
            def u_to_v(g, par):
                dve.wait_ge(ulo_ready, g + 1)
                rows = rows_of_b(par)
                nc.vector.scalar_tensor_tensor(out=u_sum[rows, :], in0=UB[0:N, :], scalar=bs_c, in1=u_lo[:],
                                               op0=ALU.add, op1=ALU.add).then_inc(usum_ready, 1)
                dve.wait_ge(usum_ready, g + 1)
                cols = bass.ds(g * (G * BATCH), G * BATCH)
                nc.vector.tensor_tensor(v_f[N:P].rearrange("p t b -> p (t b)"), u_sum[rows, :], bc[rows, cols], ALU.mult)\
                  .then_inc(v_ready, 1)
                dve.wait_ge(v_ready, g + 1)

            def state(g, s):
                if isinstance(g, int) and g == 0 and s == 0:
                    nc.vector.tensor_copy(s_f[N:P, 0], v_f[N:P, 0]).then_inc(s_ready, 1)
                else:
                    dve.wait_ge(s_ready, G * g + s)
                    nc.vector.scalar_tensor_tensor(out=s_f[N:P, s], in0=s_f[N:P, (s - 1) % G], scalar=decay,
                                                   in1=v_f[N:P, s], op0=ALU.mult, op1=ALU.add).then_inc(s_ready, 1)

            def state_to_y(g):
                dve.wait_ge(s_ready, G * (g + 1))
                dve.wait_ge(c_ready, g + 1)
                nc.vector.tensor_tensor(y_f[N:P, :], s_f[N:P].rearrange("p t b -> p (t b)"), c_f[N:P, :], ALU.mult)\
                  .then_inc(y_ready, 1)

            def y_rest(g):
                dve.wait_ge(yhi_ready, g + 1)
                nc.vector.tensor_tensor(y_hl[0:N, :], y_f[N:P, :], f(y_hl[N:P, :]), ALU.subtract).then_inc(ylo_ready, 1)

            def x1_sum(g, par, chunks):
                if 0 in chunks:
                    if isinstance(g, int):
                        wait(dve, stored[par], DMA * ((g - par) // 2))
                    else:
                        dve.wait_ge(stored[par], (g - par) * (DMA // 2))
                for c in chunks:
                    dve.wait_ge(wo_done, KC * g + c + 1)
                    nc.vector.scalar_tensor_tensor(out=x1_f[:, par, c].rearrange("p t b -> p (t b)"), in0=XB[c][:],
                                                   scalar=bo_c[:, c:c + 1],
                                                   in1=x_f[:, par, c].rearrange("p t b -> p (t b)"),
                                                   op0=ALU.add, op1=ALU.add).then_inc(x1_ready, 1)

            u_to_v(0, 0)
            for s in range(G):
                state(0, s)
            state_to_y(0)
            soft_sum(PAIRS - 2, 0, soft[(PAIRS - 2) % 4])
            y_rest(0)
            soft_sum(PAIRS - 2, 1, soft[(PAIRS - 2) % 4])
            x1_sum(0, 0, range(KC))
            for c in range(KC // 2):
                dve.wait_ge(x1hi_ready, c + 1)
                nc.vector.tensor_tensor(x1_lo[:, c], x1_f[:, 0, c], f(x1_hi[:, c]), ALU.subtract).then_inc(x1lo_ready, 1)

            def steps(g, par, first, last):
                for s in range(G):
                    t = g * G + s
                    turned_h = HB[s % 2][:].rearrange("p (c b) -> p c b", c=KC)
                    dve.wait_ge(z_done, t + 1)
                    nc.vector.tensor_tensor(z_f[:], ZB[s % 2][:], b_rows[:], ALU.add).then_inc(zsum_ready, 1)
                    if s == 2 and not last:
                        y_rest(g + 1)
                    dve.wait_ge(hthi_ready, t + 2)
                    nc.vector.tensor_tensor(hT_lo[:], turned_h, f(hT_hi[:]), ALU.subtract).then_inc(htlo_ready, 1)
                    if s == 2 and not last:
                        x1_sum(g + 1, 1 - par, range(0, 2))
                    nc.vector.tensor_tensor(x1_f[:, par, :, s, :], turned_h, x1_f[:, par, :, s, :], ALU.add)\
                      .then_inc(out_ready, 1)
                    if last:
                        continue
                    if s == 0:
                        u_to_v(g + 1, 1 - par)
                        state(g + 1, 0)
                        state(g + 1, 1)
                    if s == 1:
                        state(g + 1, 2)
                        state(g + 1, 3)
                        state_to_y(g + 1)
                    if s == 2:
                        x1_sum(g + 1, 1 - par, range(2, KC))

            groups(dve, steps)

        @block.tensor
        def _(pe):
            pe.wait_ge(ident_ready, 1)

            def convolution(c):
                for d in range(P):
                    slot, m = (d // CH) % RING, d // PER_BANK
                    if d % CH == 0:
                        pe.wait_ge(ring_loaded[slot], 2 * DMA * (P // CH // RING) * c + 2 * DMA * (d // CH // RING + 1))
                    if d % PER_BANK == 0 and m >= 4:
                        if m % 2 == 0:
                            pe.wait_ge(conv_copied_act, BANKS // 2 * c + (m - 4) // 2 + 1)
                        else:
                            pe.wait_ge(conv_copied_dve, BANKS // 2 * c + (m - 4) // 2 + 1)
                    mm = nc.tensor.matmul(CONV[m % 4][:, bass.ts(d % PER_BANK, TIME)], x_ring[:, slot, d % CH],
                                          t_ring[:, slot, d % CH], start=True, stop=True)
                    if d % PER_BANK == PER_BANK - 1:
                        mm.then_inc(conv_done, 1)

            def projection(c):
                pe.wait_ge(conv_copied_act, BANKS // 2 * (c + 1))
                pe.wait_ge(conv_copied_dve, BANKS // 2 * (c + 1))
                pe.wait_ge(wp_loaded, DMA * (c + 1))
                for m in range(BANKS + LAG):
                    if m < BANKS:
                        for i in range(PER_BANK):
                            mm = nc.tensor.transpose(TURN[m % 4][:, bass.ts(i, P)], conv[:, m * PER_BANK + i], ident[:])
                        mm.then_inc(turn_done, 1)
                    if m >= LAG:
                        n = m - LAG
                        pe.wait_ge(turn_copied, BANKS * c + n + 1)
                        if n >= 4:
                            pe.wait_ge(proj_added, BANKS * c + n - 3)
                        nc.tensor.matmul(PROJ[n % 4][:], wp_now[:, bass.ts(n % 2, P)], turned[:, n % 4], start=True, stop=True)\
                          .then_inc(proj_done, 1)

            with pe.Fori(0, KC - 1) as c:
                convolution(c)
                projection(c)
                pe.wait_ge(proj_added, BANKS * (c + 1) - 2)
            convolution(KC - 1)
            projection(KC - 1)

            def u_first(g):
                pe.wait_ge(xhi_ready, g + 1)
                wait(pe, x1_ready, KC * g)
                for k in range(KC):
                    nc.tensor.matmul(UB[:], ws_hl[:, k], x_hi[:, k], start=(k == 0), stop=False)

            def u_second(g):
                pe.wait_ge(xlo_ready, g + 1)
                for k in range(KC):
                    mm = nc.tensor.matmul(UB[:], ws_hl[:, k], x_lo[:, k], start=False, stop=(k == KC - 1))
                mm.then_inc(u_done, 1)

            def wo_product(g):
                pe.wait_ge(yhi_ready, g + 1)
                pe.wait_ge(ylo_ready, g + 1)
                for c in range(KC):
                    nc.tensor.matmul(XB[c][:], wo_hi[:, bass.ts(c, P)], y_hl[:], start=True, stop=False)
                    nc.tensor.matmul(XB[c][:], wo_lo[:, bass.ts(c, P)], y_hl[:], start=False, stop=True)\
                      .then_inc(wo_done, 1)

            def z_first(s, after=None):
                z = ZB[s % 2][:]
                for k in range(KC):
                    if after is not None:
                        pe.wait_ge(x1hi_ready, after + k + 1)
                    nc.tensor.matmul(z, x1_hi[:, k, s], wx_hi[:, k], start=(k == 0), stop=False)
                    nc.tensor.matmul(z, x1_hi[:, k, s], wx_lo[:, k], start=False, stop=False)

            def z_second(s, stop=False):
                z = ZB[s % 2][:]
                for k in range(KC):
                    mm = nc.tensor.matmul(z, x1_lo[:, k, s], wx_hi[:, k], start=False, stop=stop and k == KC - 1)
                return mm

            def z_recur(t, s, stop=True):
                z = ZB[s % 2][:]
                pe.wait_ge(hthi_ready, t + 1)
                for k in range(KC):
                    nc.tensor.matmul(z, hT_hi[:, k], wh_hi[:, k], start=False, stop=False)
                    nc.tensor.matmul(z, hT_hi[:, k], wh_lo[:, k], start=False, stop=False)
                pe.wait_ge(htlo_ready, t + 1)
                for k in range(KC):
                    mm = nc.tensor.matmul(z, hT_lo[:, k], wh_hi[:, k], start=False, stop=stop and k == KC - 1)
                return mm

            pe.wait_ge(weights_ready, 2)
            u_first(0)
            u_second(0)
            wo_product(0)
            pe.wait_ge(weights_ready, 4)
            z_first(0, after=0)
            z_recur(0, 0, stop=False)
            u_first(1)
            pe.wait_ge(x1lo_ready, KC)
            z_second(0, stop=True).then_inc(z_done, 1)

            def steps(g, par, first, last):
                for s in range(G):
                    t = g * G + s
                    end = last and s == G - 1
                    ahead = (s + 1) % G
                    if not end:
                        z_first(ahead, after=KC * (g + 1) if ahead == 0 else None)
                    pe.wait_ge(h_ready, t + 1)
                    for k in range(KC):
                        mm = nc.tensor.transpose(HB[s % 2][:, bass.ts(k, P)], h_f[:, bass.ts(k, P)], ident[:])
                    mm.then_inc(ht_done, 1)
                    if end:
                        continue
                    if s == 0 and not last:
                        u_second(g + 1)
                    if s == 3 and not (isinstance(g, int) and g == GROUPS - 2):
                        u_first(g + 2)
                    if ahead == 0:
                        pe.wait_ge(x1lo_ready, KC * (g + 2))
                    z_second(ahead)
                    if s == 2 and not last:
                        wo_product(g + 1)
                    z_recur(t + 1, ahead).then_inc(z_done, 1)

            groups(pe, steps)


def kernel(**inputs):
    import numpy as np
    import concourse.bacc as bacc
    from concourse.bass_utils import run_bass_kernel_spmd

    x = np.asarray(inputs["x"])
    cond = np.asarray(inputs["cond_1024"])
    zeros = np.zeros((D, TIME - 1), cond.dtype)
    Wp, bp, bo = (np.asarray(inputs[name]) for name in ("L0_cond_Wp", "L0_cond_bp", "L0_cond_bo"))
    other = np.r_[N:P, 0:N]

    def halves(a):
        return np.concatenate([a, a], axis=0)

    arrays = {
        "x_rev": x.transpose(1, 2, 0)[::-1],
        "x_dtb": x.transpose(2, 1, 0),
        "hankel": np.concatenate([zeros, cond[::-1].T, zeros[:, :1]], axis=1),
        "h0_t": cond.T,
        "vectors": np.concatenate([bo.reshape(KC, P).T, np.stack([bp, bp[other]], axis=1),
                                   np.stack([halves(inputs[name]) for name in
                                             ("L0_cond_bs", "L0_cond_A_log", "L0_cond_dt_log")], axis=1)], axis=1),
        "Wp": np.concatenate([Wp, Wp[:, other], np.asarray(inputs["L0_cond_conv_b"])[:, None]], axis=1),
        "Ws": inputs["L0_cond_Ws"],
        "Wo": halves(inputs["L0_cond_Wo"]),
        "Wx": inputs["L1_cond_Wx"],
        "Wh": inputs["L1_cond_Wh"],
        "b": inputs["L1_cond_b"],
    }
    arrays = {name: np.ascontiguousarray(a) for name, a in arrays.items()}
    nc = bacc.Bacc("TRN2", target_bir_lowering=False, num_devices=1)
    args = {
        name: nc.dram_tensor(name, a.shape, mybir.dt.from_np(a.dtype), kind="ExternalInput").ap()
        for name, a in arrays.items()
    }
    out = nc.dram_tensor("out", (D, TIME, BATCH), F32, kind="ExternalOutput").ap()
    build(nc, **args, out=out)
    result = run_bass_kernel_spmd(nc, [arrays], core_ids=[0])
    return result.results[0]["out"].transpose(2, 1, 0)
```
